# Optimizing a Trainium2 kernel written in Bass

```python
import numpy as np
import jax
import jax.numpy as jnp

def _softmax(x, axis=-1):
    return jax.nn.softmax(x, axis=axis)

def _gelu(x):
    return jax.nn.gelu(x, approximate=True)

def _silu(x):
    return jax.nn.silu(x)

def _sigmoid(x):
    return jax.nn.sigmoid(x)

def _layernorm(x, axis=-1, eps=1e-05):
    m = jnp.mean(x, axis=axis, keepdims=True)
    v = jnp.var(x, axis=axis, keepdims=True)
    return (x - m) / jnp.sqrt(v + eps)

def _scatter_add(tgt, idx, src, axis=0):
    return tgt.at[idx].add(src)

def _segment_sum(src, seg, n):
    return jax.ops.segment_sum(src, seg, n)
kernel_name = 'mk_adj_resnorm_d1_adj_r2_8bceb8'

def setup_inputs(seed: int=0):
    np.random.seed(seed)
    _w = jnp.asarray

    def _rec_inputs():
        import jax
        import jax.numpy as jnp
        _gk = jax.random.key(seed)
        x = -0.0004039 + 1 * jax.random.normal(jax.random.fold_in(_gk, 1), (32, 256, 384), jnp.float32)
        _a = jax.random.bernoulli(jax.random.fold_in(_gk, 2), 0.0625, (32, 256, 256))
        _af = _a.astype(jnp.float32)
        adj = _af
        return (x, adj)
    x, adj = _rec_inputs()

    def _L0_gnn_setup():
        import jax, jax.numpy as jnp
        import numpy as np
        B, S, H, L = (32, 256, 384, 2)

        def _layer_norm(z, a, b, eps=0.001):
            mu = jnp.mean(z, axis=-1, keepdims=True)
            sigma = jnp.std(z, axis=-1, keepdims=True, ddof=1)
            return (z - mu) / (sigma + eps) * a + b
        key = jax.random.key(seed)
        ks = jax.random.split(key, 6)
        hidden_state = jax.random.normal(ks[0], (B, S, H), dtype=jnp.float32)
        adjacency_matrix = (jax.random.uniform(ks[1], (B, S, S)) < 0.2).astype(jnp.float32)
        W_left = 0.05 * jax.random.normal(ks[2], (L, H, H), dtype=jnp.float32)
        W_right = 0.05 * jax.random.normal(ks[3], (L, H, H), dtype=jnp.float32)
        W_lin = 0.05 * jax.random.normal(ks[4], (L, H, H), dtype=jnp.float32)
        b_lin = jnp.zeros((L, H), dtype=jnp.float32)
        ln_a = jnp.ones((L, H), dtype=jnp.float32)
        ln_b = jnp.zeros((L, H), dtype=jnp.float32)
        return {'hidden_state': hidden_state, 'adjacency_matrix': adjacency_matrix, 'W_left': W_left, 'W_right': W_right, 'W_lin': W_lin, 'b_lin': b_lin, 'ln_a': ln_a, 'ln_b': ln_b}
    _L0_gnn_all = _L0_gnn_setup()
    _L0_gnn_in = {k: v for k, v in _L0_gnn_all.items() if k in ('W_left', 'W_right', 'W_lin', 'b_lin', 'ln_a', 'ln_b')}
    del _L0_gnn_all
    return {'x': x, 'adj': adj, 'L0_gnn_W_left': _L0_gnn_in['W_left'], 'L0_gnn_W_right': _L0_gnn_in['W_right'], 'L0_gnn_W_lin': _L0_gnn_in['W_lin'], 'L0_gnn_b_lin': _L0_gnn_in['b_lin'], 'L0_gnn_ln_a': _L0_gnn_in['ln_a'], 'L0_gnn_ln_b': _L0_gnn_in['ln_b']}

def reference(x, adj, L0_gnn_W_left, L0_gnn_W_right, L0_gnn_W_lin, L0_gnn_b_lin, L0_gnn_ln_a, L0_gnn_ln_b):
    import jax
    import jax.numpy as jnp

    def _L0_gnn_ref(hidden_state, adjacency_matrix, W_left, W_right, W_lin, b_lin, ln_a, ln_b):
        import jax, jax.numpy as jnp
        import numpy as np
        B, S, H, L = (32, 256, 384, 2)

        def _layer_norm(z, a, b, eps=0.001):
            mu = jnp.mean(z, axis=-1, keepdims=True)
            sigma = jnp.std(z, axis=-1, keepdims=True, ddof=1)
            return (z - mu) / (sigma + eps) * a + b
        temper = float(np.sqrt(H))
        adj = adjacency_matrix
        adj_tri = jnp.triu(adj, k=1)
        diag_mask = jnp.triu(adj, k=0) - adj_tri
        h = hidden_state
        for l in range(L):
            m_left = jnp.einsum('bsh,oh->bso', h, W_left[l])
            m_right = jnp.einsum('bsh,oh->bso', h, W_right[l])
            u_left = jnp.einsum('bih,bjh->bij', h, m_left) / temper
            u_right = jnp.einsum('bih,bjh->bij', h, m_right) / temper
            u = u_left * adj_tri + u_left * diag_mask + u_right * jnp.swapaxes(adj_tri, 1, 2)
            delta_exp_u = jnp.exp(u) * adj
            attention = delta_exp_u / (jnp.sum(delta_exp_u, axis=2, keepdims=True) + 1e-10)
            h_lin = jnp.einsum('bsh,oh->bso', h, W_lin[l]) + b_lin[l]
            ctx = jnp.matmul(attention, h_lin)
            h = jax.nn.relu(_layer_norm(ctx, ln_a[l], ln_b[l]))
        return h
    x = _layernorm(x + _L0_gnn_ref(x, adj, L0_gnn_W_left, L0_gnn_W_right, L0_gnn_W_lin, L0_gnn_b_lin, L0_gnn_ln_a, L0_gnn_ln_b), axis=-1)
    return x

_drawn_inputs = setup_inputs


def setup_inputs(seed=0):
    import zlib

    import numpy as np

    out = dict(_drawn_inputs(seed))
    spreads = {'L0_gnn_b_lin': (0.0, 0.1), 'L0_gnn_ln_a': (1.0, 0.2), 'L0_gnn_ln_b': (0.0, 0.1)}
    factors = {}
    for name, (base, spread) in spreads.items():
        noise = np.random.default_rng([zlib.crc32(name.encode()), seed]).standard_normal(out[name].shape)
        drawn = base * np.exp(spread * noise) if base else spread * noise
        out[name] = jnp.asarray(drawn.astype(out[name].dtype))
    for name, factor in factors.items():
        out[name] = (out[name] * factor).astype(out[name].dtype)
    return out
```

```python
from contextlib import ExitStack

import concourse.bass as bass
from concourse import mybir

F32 = mybir.dt.float32
F32R = mybir.dt.float32r
ALU = mybir.AluOpType
ACT = mybir.ActivationFunctionType

P = 128
PAIR = 2
PHASES = 4
LN_EPS = 1e-3
SUM_EPS = 1e-10
OUT_EPS = 1e-5
PASSES = (("hi", "hi"), ("lo", "hi"), ("hi", "lo"))


class Slot:

    def __init__(self, pair, phase):
        self.pair, self.phase = pair, phase
        self.parity = phase % PAIR
        self.layer = phase // PAIR
        self.batch = pair * PAIR + self.parity

    def shift(self, d):
        return Slot(self.pair + (self.phase + d) // PHASES, (self.phase + d) % PHASES)

    def done(self, per_slot, k):
        n = self.pair * (PHASES * per_slot) + (self.phase * per_slot + k)
        return max(n, 0) if isinstance(n, int) else n

    def done_batch(self, per_batch, k):
        n = self.pair * (PAIR * per_batch) + (self.parity * per_batch + k)
        return max(n, 0) if isinstance(n, int) else n

    def done_own(self, per, k):
        n = self.pair * per + k
        return max(n, 0) if isinstance(n, int) else n


def build(nc, x, adj, w_left, w_right, w_lin, b_lin, ln_a, ln_b, out):
    B, S, H = x.shape
    L = w_left.shape[0]
    NS, NH = S // P, H // P
    assert S == 2 * P and H == 3 * P and L == 2 and B % PAIR == 0
    PAIRS = B // PAIR
    TEMPER = float(H) ** 0.5
    SCORES = 3 * P
    HL = H + 2
    DDOF = (H / (H - 1.0)) ** 0.5

    with ExitStack() as ctx:
        def sb(name, shape, dt=F32):
            return ctx.enter_context(nc.sbuf_tensor(name, shape, dt))

        def bank(name, shape):
            return ctx.enter_context(nc.psum_tensor(name, shape, F32))

        def sem(name):
            return ctx.enter_context(nc.semaphore(name))

        def parts(name, shape):
            return {"hi": sb(name + "_hi", shape, F32R), "lo": sb(name + "_lo", shape, F32R)}

        wr = parts("wr", [P, L, NH, H])
        wl = parts("wl", [P, L, NH, H])
        wt = parts("wt", [P, L, NH, H])
        w_stage = sb("w_stage", [P, 3, NH, H])
        b_row = sb("b_row", [P, L, H])
        a_row = sb("a_row", [P, H])
        c_row = sb("c_row", [P, H])
        a_col = sb("a_col", [P, NH])
        c_col = sb("c_col", [P, NH])
        ident = sb("ident", [P, P])
        later = sb("later", [P, NS, P])
        not_later = sb("not_later", [P, NS, P])
        half = sb("half", [P, NS])
        neg_half = sb("neg_half", [P, NS])
        x_stage = sb("x_stage", [P, PAIR, NS, H])
        x_res = sb("x_res", [P, PAIR, NS, H])
        adj_stage = sb("adj_stage", [P, PAIR, NS, S])
        mask = sb("mask", [P, PAIR, NS, SCORES])
        adj_t = sb("adj_t", [P, PAIR, NS, S])
        ht = parts("ht", [P, PAIR, NH, S])
        hl = parts("hl", [P, PAIR, NS, HL])
        y = sb("y", [P, PAIR, NS, H])
        h_full = sb("h_full", [P, NH, S])
        g = parts("g", [P, NH, 2 * S])
        hl_full = sb("hl_full", [P, NS, H])
        masked = sb("masked", [P, NS, SCORES])
        expd = sb("expd", [P, NS, S])
        p_full = sb("p_full", [P, NS, S])
        pt = parts("pt", [P, NS, S])
        z = sb("z", [P, NS, H])
        stats = sb("stats", [P, NS, 6])
        moments = sb("moments", [P, NS, 2])
        sum_eps = sb("sum_eps", [P, NS])
        std = sb("std", [P, NS])
        denom = sb("denom", [P, NS])
        inv_std = sb("inv_std", [P, NS])
        shift = sb("shift", [P, NS])
        out_stats = sb("out_stats", [P, NS, 6])
        out_moments = sb("out_moments", [P, NS, 2])
        out_var = sb("out_var", [P, NS])
        out_inv = sb("out_inv", [P, PAIR, NS])
        out_mean = sb("out_mean", [P, PAIR, NS])
        out_shift = sb("out_shift", [P, NS])

        proj = [bank(f"proj{c}", [P, 2 * S]) for c in range(NH)]
        score = [bank(f"score{j}", [P, 2 * S]) for j in range(NS)]
        ctx_ps = bank("ctx_ps", [P, NS, 2 * S])
        tr = bank("tr", [P, 2 * S])
        tr_bank = [tr[:, 0:S], ctx_ps[:, 0, 0:S], ctx_ps[:, 1, 0:S]]

        w_loaded = [[sem(f"w{l}{n}_loaded") for n in ("right", "left", "lin")] for l in range(L)]
        rows_loaded = sem("rows_loaded")
        x_loaded = [sem(f"x_loaded{p}") for p in range(PAIR)]
        adj_loaded = [sem(f"adj_loaded{p}") for p in range(PAIR)]
        x_copied = [sem(f"x_copied{p}") for p in range(PAIR)]
        stored = [sem(f"stored{p}") for p in range(PAIR)]
        consts_ready = sem("consts_ready")
        ident_filled = sem("ident_filled")
        ones_ready = sem("ones_ready")
        wt_done = sem("wt_done")
        w_hi_ready = sem("w_hi_ready")
        w_lo_ready = sem("w_lo_ready")
        transposed = sem("transposed")
        h_full_ready = sem("h_full_ready")
        ht_hi_ready = sem("ht_hi_ready")
        ht_lo_ready = sem("ht_lo_ready")
        g_done = sem("g_done")
        g_hi_ready = sem("g_hi_ready")
        g_lo_ready = sem("g_lo_ready")
        hl_done = sem("hl_done")
        hl_full_ready = sem("hl_full_ready")
        hl_hi_ready = sem("hl_hi_ready")
        hl_lo_ready = sem("hl_lo_ready")
        score_done = sem("score_done")
        masked_ready = sem("masked_ready")
        summed_ready = sem("summed_ready")
        exp_ready = sem("exp_ready")
        p_full_ready = sem("p_full_ready")
        p_hi_ready = sem("p_hi_ready")
        p_lo_ready = sem("p_lo_ready")
        ctx_done = sem("ctx_done")
        stats_ready = sem("stats_ready")
        moments_ready = sem("moments_ready")
        std_ready = sem("std_ready")
        denom_ready = sem("denom_ready")
        inv_ready = sem("inv_ready")
        shift_ready = sem("shift_ready")
        adj_done = sem("adj_done")
        adj_t_ready = sem("adj_t_ready")
        mask_ready = sem("mask_ready")
        z_ready = sem("z_ready")
        centred_ready = sem("centred_ready")
        scaled_ready = sem("scaled_ready")
        resid_ready = sem("resid_ready")
        out_stats_ready = sem("out_stats_ready")
        out_moments_ready = sem("out_moments_ready")
        out_var_ready = sem("out_var_ready")
        out_inv_ready = sem("out_inv_ready")
        out_shift_ready = sem("out_shift_ready")
        out_ready = sem("out_ready")

        def element(dram, b):
            size = dram.shape[1] * dram.shape[2]
            flat = dram.rearrange("b s h -> (b s h)")[bass.ds(b * size, size)]
            return flat.rearrange("(n p h) -> p n h", p=P, h=dram.shape[2])

        def ahead(eng, dram, b, *counts):
            for value in (b * (dram.shape[1] * dram.shape[2] * 4), *counts):
                if not isinstance(value, int):
                    eng.to_reg(value)

        block = ctx.enter_context(nc.Block())

        def run_slots(eng, slot, first, last):
            first()
            for phase in (0, 1):
                slot(Slot(0, phase), at_start=(phase == 0), at_end=False)
            with eng.Fori(0, PAIRS - 1) as pair:
                for phase in (2, 3):
                    slot(Slot(pair, phase), at_start=False, at_end=False)
                for phase in (0, 1):
                    slot(Slot(pair + 1, phase), at_start=False, at_end=False)
            for phase in (2, 3):
                slot(Slot(PAIRS - 1, phase), at_start=False, at_end=(phase == 3))
            last()

        LAST = Slot(PAIRS - 1, PHASES - 1)

        @block.sync
        def _(sp):
            def load(b, parity):
                sp.dma_start(x_stage[:, parity], element(x, b)).then_inc(x_loaded[parity], 16)
                sp.dma_start(adj_stage[:, parity], element(adj, b)).then_inc(adj_loaded[parity], 16)

            def first():
                load(0, 0)
                for n, w in enumerate((w_right, w_left, w_lin)):
                    sp.dma_start(w_stage[:, n], w[0].rearrange("(k p) h -> p k h", p=P)).then_inc(w_loaded[0][n], 16)
                load(1, 1)
                sp.wait_ge(w_lo_ready, 5)
                for n, w in enumerate((w_right, w_left, w_lin)):
                    sp.dma_start(w_stage[:, n], w[1].rearrange("(k p) h -> p k h", p=P)).then_inc(w_loaded[1][n], 16)

            def slot(s, at_start, at_end):
                p = s.parity
                if s.layer == 0:
                    if not at_end:
                        ahead(sp, x, s.batch + PAIR, s.done_own(16, 16), s.done_batch(NS, -NS),
                              s.done(NH, NH), s.done_batch(1, 1))
                        ahead(sp, adj, s.batch + PAIR)
                    sp.wait_ge(x_loaded[p], s.done_own(16, 16))
                    sp.wait_ge(resid_ready, s.done_batch(NS, -NS))
                    sp.dma_start(x_res[:, p], x_stage[:, p]).then_inc(x_copied[p], 16)
                    if at_end:
                        return
                    sp.wait_ge(x_copied[p], s.done_own(16, 16))
                    sp.wait_ge(transposed, s.done(NH, NH))
                    sp.wait_ge(mask_ready, s.done_batch(1, 1))
                    sp.dma_start(x_stage[:, p], element(x, s.batch + PAIR)).then_inc(x_loaded[p], 16)
                    sp.dma_start(adj_stage[:, p], element(adj, s.batch + PAIR)).then_inc(adj_loaded[p], 16)

            def store(s):
                p = s.parity
                ahead(sp, out, s.batch, s.done_batch(NS, NS))
                sp.wait_ge(out_ready, s.done_batch(NS, NS))
                sp.dma_start(element(out, s.batch), y[:, p]).then_inc(stored[p], 16)

            first()
            for phase in (0, 1):
                slot(Slot(0, phase), phase == 0, False)
            with sp.Fori(0, PAIRS - 2) as pair:
                for phase in (0, 1):
                    slot(Slot(pair + 1, phase), False, False)
                    store(Slot(pair, phase))
            for phase in (0, 1):
                slot(Slot(PAIRS - 1, phase), False, True)
                store(Slot(PAIRS - 2, phase))
            for phase in (0, 1):
                store(Slot(PAIRS - 1, phase))
            for p in range(PAIR):
                sp.wait_ge(stored[p], 16 * PAIRS)

        @block.tensor
        def _(pe):
            def transpose_lin(l):
                pe.wait_ge(w_loaded[l][2], 16)
                for k in range(NH):
                    if l:
                        pe.wait_ge(hl_full_ready if k < NS else g_lo_ready, k + 1)
                    for o in range(NH):
                        last = nc.tensor.transpose(proj[k][:, o * P:(o + 1) * P],
                                                   w_stage[:, 2, o, k * P:(k + 1) * P], ident[:, :])
                    last.then_inc(wt_done, 1)

            def transpose_h(s):
                if s.layer == 0:
                    pe.wait_ge(x_loaded[s.parity], s.done_own(16, 16))
                    pe.wait_ge(centred_ready, s.done_batch(NS, -NS))
                    src = x_stage[:, s.parity]
                else:
                    pe.wait_ge(z_ready, s.done_batch(NS, NS))
                    src = z
                for k in range(NH):
                    if k == 0:
                        pe.wait_ge(ht_lo_ready, s.done(NH, 1 - NH))
                    for i in range(NS):
                        last = nc.tensor.transpose(tr_bank[k][:, i * P:(i + 1) * P],
                                                   src[:, i, k * P:(k + 1) * P], ident[:, :])
                    last.then_inc(transposed, 1)

            def project(s, c):
                if c < NS:
                    pe.wait_ge(hl_full_ready, s.done(NS, c + 1 - NS))
                for w, at in ((wr, 0), (wl, S)):
                    for k in range(NH):
                        for n, (a, b) in enumerate(PASSES):
                            if c == 0 and at == 0 and n == 0:
                                pe.wait_ge(ht_hi_ready, s.done(NH, k + 1))
                            if c == 0 and at == 0 and n == 2:
                                pe.wait_ge(ht_lo_ready, s.done(NH, k + 1))
                            last = nc.tensor.matmul(proj[c][:, at:at + S],
                                                    w[a][:, s.layer, k, c * P:(c + 1) * P],
                                                    ht[b][:, s.parity, k, :],
                                                    start=(k == 0 and n == 0), stop=(k == NH - 1 and n == 2))
                last.then_inc(g_done, 1)

            def linear(s, i):
                pe.wait_ge(g_lo_ready, s.done(NH, i + 1))
                for k in range(NH):
                    for n, (a, b) in enumerate(PASSES):
                        last = nc.tensor.matmul(proj[i][:, 0:H], ht[a][:, s.parity, k, i * P:(i + 1) * P],
                                                wt[b][:, s.layer, k, :],
                                                start=(k == 0 and n == 0), stop=(k == NH - 1 and n == 2))
                last.then_inc(hl_done, 1)

            def scores(s, j):
                if j == 0:
                    pe.wait_ge(g_lo_ready, s.done(NH, NH))
                    pe.wait_ge(adj_t_ready, s.done_batch(1, 1))
                pe.wait_ge(masked_ready, s.done(NS, j + 1 - NS))
                for k in range(NH):
                    for n, (a, b) in enumerate(PASSES):
                        last = nc.tensor.matmul(score[j][:, 0:SCORES], ht[a][:, s.parity, k, j * P:(j + 1) * P],
                                                g[b][:, k, j * P:j * P + SCORES],
                                                start=(k == 0 and n == 0), stop=(k == NH - 1 and n == 2))
                last.then_inc(score_done, 1)

            def context(s, i):
                if i == 0:
                    pe.wait_ge(p_lo_ready, s.done(NS, NS))
                    pe.wait_ge(hl_lo_ready, s.done(NS, NS))
                    if s is not LAST:
                        pe.wait_ge(ht_lo_ready, s.done(NH, 2 * NH))
                for j in range(NS):
                    q = i if j == 0 else 1 - i
                    for n, (a, b) in enumerate(PASSES):
                        wide = HL if b == "hi" else H
                        last = nc.tensor.matmul(ctx_ps[:, i, 0:wide], pt[a][:, j, q * P:(q + 1) * P],
                                                hl[b][:, s.parity, j, 0:wide],
                                                start=(j == 0 and n == 0), stop=(j == NS - 1 and n == 2))
                last.then_inc(ctx_done, 1)

            def transpose_adj(s):
                pe.wait_ge(adj_loaded[s.parity], s.done_own(16, 16))
                pe.wait_ge(masked_ready, s.done(NS, -NS - 1))
                for j in range(NS):
                    for n in range(NS):
                        i = n if j == 0 else 1 - n
                        last = nc.tensor.transpose(score[0][:, (2 * j + n) * P:(2 * j + n + 1) * P],
                                                   adj_stage[:, s.parity, i, j * P:(j + 1) * P], ident[:, :])
                last.then_inc(adj_done, 1)

            def slot(s, at_start, at_end):
                prev, nxt = s.shift(-1), s.shift(1)
                project(s, 0)
                project(s, 1)
                if not at_start:
                    context(prev, 0)
                    context(prev, 1)
                if not at_end and nxt.layer == 0:
                    transpose_adj(nxt)
                project(s, 2)
                for i in range(NS):
                    linear(s, i)
                if not at_end:
                    transpose_h(nxt)
                scores(s, 0)
                scores(s, 1)
                if at_start:
                    transpose_lin(1)
                    pe.wait_ge(w_lo_ready, 10)

            def first():
                pe.wait_ge(consts_ready, 1)
                pe.wait_ge(ones_ready, PAIR * NS)
                transpose_h(Slot(0, 0))
                transpose_adj(Slot(0, 0))
                transpose_lin(0)
                pe.wait_ge(w_lo_ready, 5)

            def last():
                for i in range(NS):
                    context(LAST, i)

            run_slots(pe, slot, first, last)

        @block.scalar
        def _(act):
            def prepare(l):
                for n, w in enumerate((wr, wl)):
                    act.wait_ge(w_loaded[l][n], 16)
                    nc.scalar.copy(w["hi"][:, l], w_stage[:, n]).then_inc(w_hi_ready, 1)
                for k in range(NH):
                    act.wait_ge(wt_done, NH * l + k + 1)
                    nc.scalar.copy(wt["hi"][:, l, k, :], proj[k][:, 0:H]).then_inc(w_hi_ready, 1)

            def take_h(s):
                act.wait_ge(score_done, s.done(NS, -NS))
                for k in range(NH):
                    act.wait_ge(transposed, s.done(NH, k + 1))
                    if s.layer == 0:
                        nc.scalar.copy(ht["hi"][:, s.parity, k, :], tr_bank[k]).then_inc(ht_hi_ready, 1)
                    else:
                        nc.scalar.activation(h_full[:, k, :], tr_bank[k], ACT.Relu, bias=c_col[:, k:k + 1],
                                             scale=a_col[:, k:k + 1]).then_inc(h_full_ready, 1)

            def take_g(s, c):
                act.wait_ge(g_done, s.done(NH, c + 1))
                act.wait_ge(score_done, s.done(NS, 0))
                nc.scalar.copy(g["hi"][:, c, :], proj[c][:, :]).then_inc(g_hi_ready, 1)

            def take_hl(s, i):
                act.wait_ge(hl_full_ready, s.done(NS, i + 1))
                act.wait_ge(ctx_done, s.done(NS, -NS))
                nc.scalar.copy(hl["hi"][:, s.parity, i, 0:H], hl_full[:, i, :]).then_inc(hl_hi_ready, 1)

            def exponent(s, j):
                act.wait_ge(summed_ready, s.done(NS, j + 1))
                act.wait_ge(p_full_ready, s.done(NS, j + 1 - NS))
                nc.scalar.activation(expd[:, j, :], masked[:, j, 0:S], ACT.Exp,
                                     scale=1.0 / TEMPER).then_inc(exp_ready, 1)

            def take_p(s, j):
                act.wait_ge(p_full_ready, s.done(NS, j + 1))
                act.wait_ge(ctx_done, s.done(NS, 0))
                nc.scalar.copy(pt["hi"][:, j, :], p_full[:, j, :]).then_inc(p_hi_ready, 1)

            def normalise(s):
                act.wait_ge(shift_ready, s.done(1, 1))
                act.wait_ge(transposed, s.done(NH, 2 * NH))
                for i in range(NS):
                    nc.scalar.activation(z[:, i, :], ctx_ps[:, i, 0:H], ACT.Identity, bias=shift[:, i:i + 1],
                                         scale=inv_std[:, i:i + 1]).then_inc(z_ready, 1)

            def finish(s):
                act.wait_ge(out_shift_ready, s.done_batch(1, 1))
                for i in range(NS):
                    nc.scalar.activation(y[:, s.parity, i, :], y[:, s.parity, i, :], ACT.Identity,
                                         bias=out_shift[:, i:i + 1],
                                         scale=out_inv[:, s.parity, i:i + 1]).then_inc(out_ready, 1)

            def take_adj(s):
                act.wait_ge(adj_done, s.done_batch(1, 1))
                act.wait_ge(p_full_ready, s.done(NS, -NS))
                nc.scalar.copy(adj_t[:, s.parity],
                               score[0][:, :].rearrange("p (j q) -> p j q", j=NS)).then_inc(adj_t_ready, 1)

            def slot(s, at_start, at_end):
                prev, before, nxt = s.shift(-1), s.shift(-2), s.shift(1)
                if not at_start:
                    exponent(prev, 1)
                    take_p(prev, 1)
                take_g(s, 0)
                take_g(s, 1)
                if not at_end and nxt.layer == 0:
                    take_adj(nxt)
                if not at_start and prev.layer == 0:
                    normalise(prev)
                take_g(s, 2)
                if before.layer == 1 and not (isinstance(s.pair, int) and s.pair == 0):
                    finish(before)
                for i in range(NS):
                    take_hl(s, i)
                if not at_end:
                    take_h(nxt)
                exponent(s, 0)
                take_p(s, 0)
                if at_start:
                    prepare(1)

            def first():
                act.dma_start(a_col[:, :], ln_a[0].rearrange("(k p) -> p k", p=P),
                              allow_slow_non_contiguous=True).then_inc(rows_loaded, 16)
                act.dma_start(c_col[:, :], ln_b[0].rearrange("(k p) -> p k", p=P),
                              allow_slow_non_contiguous=True).then_inc(rows_loaded, 16)
                for l in range(L):
                    act.dma_start(b_row[:, l, :], b_lin[l].partition_broadcast(P)).then_inc(rows_loaded, 16)
                act.dma_start(a_row[:, :], ln_a[1].partition_broadcast(P)).then_inc(rows_loaded, 16)
                act.dma_start(c_row[:, :], ln_b[1].partition_broadcast(P)).then_inc(rows_loaded, 16)
                take_h(Slot(0, 0))
                take_adj(Slot(0, 0))
                prepare(0)
                act.wait_ge(rows_loaded, 6 * 16)

            def last():
                exponent(LAST, 1)
                take_p(LAST, 1)
                finish(LAST.shift(-1))
                finish(LAST)

            run_slots(act, slot, first, last)

        @block.vector
        def _(dve):
            def prepare(l):
                for n, w in enumerate((wr, wl)):
                    dve.wait_ge(w_hi_ready, 5 * l + n + 1)
                    nc.vector.tensor_tensor(w["lo"][:, l], w_stage[:, n], w["hi"][:, l].bitcast(F32),
                                            ALU.subtract).then_inc(w_lo_ready, 1)
                for k in range(NH):
                    dve.wait_ge(w_hi_ready, 5 * l + k + 3)
                    nc.vector.tensor_tensor(wt["lo"][:, l, k, :], proj[k][:, 0:H], wt["hi"][:, l, k, :].bitcast(F32),
                                            ALU.subtract).then_inc(w_lo_ready, 1)

            def split_h(s):
                for k in range(NH):
                    hi, lo = (ht[a][:, s.parity, k, :] for a in ("hi", "lo"))
                    if s.layer == 1:
                        dve.wait_ge(h_full_ready, s.done_batch(NH, k + 1))
                        nc.vector.tensor_copy(hi, h_full[:, k, :]).then_inc(ht_hi_ready, 1)
                    dve.wait_ge(ht_hi_ready, s.done(NH, k + 1))
                    nc.vector.tensor_tensor(lo, h_full[:, k, :] if s.layer else tr_bank[k], hi.bitcast(F32),
                                            ALU.subtract).then_inc(ht_lo_ready, 1)

            def split_g(s, c):
                dve.wait_ge(g_hi_ready, s.done(NH, c + 1))
                nc.vector.tensor_tensor(g["lo"][:, c, :], proj[c][:, :], g["hi"][:, c, :].bitcast(F32),
                                        ALU.subtract).then_inc(g_lo_ready, 1)

            def add_bias(s, i):
                dve.wait_ge(hl_done, s.done(NS, i + 1))
                dve.wait_ge(hl_lo_ready, s.done(NS, i + 1 - NS))
                nc.vector.tensor_tensor(hl_full[:, i, :], proj[i][:, 0:H], b_row[:, s.layer, :],
                                        ALU.add).then_inc(hl_full_ready, 1)

            def mask_scores(s, j):
                dve.wait_ge(score_done, s.done(NS, j + 1))
                dve.wait_ge(mask_ready, s.done_batch(1, 1))
                dve.wait_ge(exp_ready, s.done(NS, j + 1 - NS))
                nc.vector.tensor_tensor(masked[:, j, :], score[j][:, 0:SCORES], mask[:, s.parity, j, :],
                                        ALU.mult).then_inc(masked_ready, 1)
                dve.wait_ge(masked_ready, s.done(NS, j + 1))
                nc.vector.tensor_tensor(masked[:, j, 0:P], masked[:, j, 0:P], masked[:, j, 2 * P:3 * P],
                                        ALU.add).then_inc(summed_ready, 1)

            def weigh(s, j):
                dve.wait_ge(exp_ready, s.done(NS, j + 1))
                nc.vector.tensor_tensor(p_full[:, j, :], expd[:, j, :], adj_t[:, s.parity, j, :],
                                        ALU.mult).then_inc(p_full_ready, 1)
                dve.wait_ge(p_hi_ready, s.done(NS, j + 1))
                nc.vector.tensor_tensor(pt["lo"][:, j, :], p_full[:, j, :], pt["hi"][:, j, :].bitcast(F32),
                                        ALU.subtract).then_inc(p_lo_ready, 1)

            def norm_scalars(s):
                for i in range(NS):
                    dve.wait_ge(ctx_done, s.done(NS, i + 1))
                    nc.vector.bn_stats(stats[:, i, :], ctx_ps[:, i, 0:H]).then_inc(stats_ready, 1)
                dve.wait_ge(stats_ready, s.done(NS, NS))
                nc.vector.tensor_scalar(sum_eps[:, :], ctx_ps[:, :, H], LN_EPS, LN_EPS * SUM_EPS, ALU.mult,
                                        ALU.add).then_inc(moments_ready, 1)
                for i in range(NS):
                    nc.vector.bn_aggr(moments[:, i, :], stats[:, i, :]).then_inc(moments_ready, 1)
                dve.wait_ge(std_ready, s.done(1, 1))
                dve.wait_ge(moments_ready, s.done(3, 3))
                nc.vector.scalar_tensor_tensor(denom[:, :], std[:, :], DDOF, sum_eps[:, :], ALU.mult,
                                               ALU.add).then_inc(denom_ready, 1)
                dve.wait_ge(denom_ready, s.done(1, 1))
                nc.vector.reciprocal(inv_std[:, :], denom[:, :]).then_inc(inv_ready, 1)
                dve.wait_ge(inv_ready, s.done(1, 1))
                if s.layer == 0:
                    nc.vector.scalar_tensor_tensor(shift[:, :], moments[:, :, 0], -1.0, inv_std[:, :], ALU.mult,
                                                   ALU.mult).then_inc(shift_ready, 1)
                else:
                    nc.vector.scalar_tensor_tensor(shift[:, :], moments[:, :, 0], -1.0, inv_std[:, :], ALU.mult,
                                                   ALU.mult).then_inc(shift_ready, 1)

            def residual(s):
                dve.wait_ge(stored[s.parity], s.done_own(16, 0))
                for i in range(NS):
                    nc.vector.scalar_tensor_tensor(y[:, s.parity, i, :], ctx_ps[:, i, 0:H], moments[:, i, 0:1],
                                                   a_row[:, :], ALU.subtract, ALU.mult).then_inc(centred_ready, 1)
                for i in range(NS):
                    yi = y[:, s.parity, i, :]
                    dve.wait_ge(centred_ready, s.done_batch(NS, i + 1))
                    nc.vector.scalar_tensor_tensor(yi, yi, inv_std[:, i:i + 1], c_row[:, :], ALU.mult,
                                                   ALU.add).then_inc(scaled_ready, 1)
                dve.wait_ge(x_copied[s.parity], s.done_own(16, 16))
                for i in range(NS):
                    yi = y[:, s.parity, i, :]
                    dve.wait_ge(scaled_ready, s.done_batch(NS, i + 1))
                    nc.vector.scalar_tensor_tensor(yi, yi, 0.0, x_res[:, s.parity, i, :], ALU.max,
                                                   ALU.add).then_inc(resid_ready, 1)
                for i in range(NS):
                    dve.wait_ge(resid_ready, s.done_batch(NS, i + 1))
                    nc.vector.bn_stats(out_stats[:, i, :], y[:, s.parity, i, :]).then_inc(out_stats_ready, 1)
                dve.wait_ge(out_stats_ready, s.done_batch(NS, NS))

            def out_variance(s):
                for i in range(NS):
                    nc.vector.bn_aggr(out_moments[:, i, :], out_stats[:, i, :]).then_inc(out_moments_ready, 1)
                dve.wait_ge(out_moments_ready, s.done_batch(NS, NS))
                dve.wait_ge(out_inv_ready, s.done_batch(1, 0))
                nc.vector.tensor_scalar(out_var[:, :], out_moments[:, :, 1], OUT_EPS, None,
                                        ALU.add).then_inc(out_var_ready, 1)
                nc.vector.tensor_copy(out_mean[:, s.parity, :], out_moments[:, :, 0]).then_inc(out_var_ready, 1)

            def out_scalars(s):
                dve.wait_ge(out_inv_ready, s.done_batch(1, 1))
                dve.wait_ge(out_ready, s.done_batch(NS, 0))
                nc.vector.scalar_tensor_tensor(out_shift[:, :], out_mean[:, s.parity, :], -1.0,
                                               out_inv[:, s.parity, :], ALU.mult,
                                               ALU.mult).then_inc(out_shift_ready, 1)

            def slot(s, at_start, at_end):
                prev, before, nxt = s.shift(-1), s.shift(-2), s.shift(1)
                if not at_start:
                    mask_scores(prev, 1)
                    weigh(prev, 1)
                split_g(s, 0)
                split_g(s, 1)
                if before.layer == 1 and not (isinstance(s.pair, int) and s.pair == 0):
                    out_scalars(before)
                if not at_start:
                    norm_scalars(prev)
                    if prev.layer == 1:
                        residual(prev)
                split_g(s, 2)
                if not at_start and prev.layer == 1:
                    out_variance(prev)
                for i in range(NS):
                    add_bias(s, i)
                if not at_end:
                    split_h(nxt)
                mask_scores(s, 0)
                weigh(s, 0)
                if at_start:
                    prepare(1)

            def first():
                ones = [hl["hi"][:, p, i, H:HL].bitcast(F32) for p in range(PAIR) for i in range(NS)]
                for t in ones:
                    nc.vector.memset(t, 1.0).then_inc(ones_ready, 1)
                split_h(Slot(0, 0))
                prepare(0)
                dve.wait_ge(rows_loaded, 6 * 16)

            def last():
                mask_scores(LAST, 1)
                weigh(LAST, 1)
                out_scalars(LAST.shift(-1))
                norm_scalars(LAST)
                residual(LAST)
                out_variance(LAST)
                out_scalars(LAST)

            run_slots(dve, slot, first, last)

        @block.gpsimd
        def _(pool):
            def deviation(s):
                pool.wait_ge(moments_ready, s.done(3, 3))
                pool.wait_ge(denom_ready, s.done(1, 0))
                nc.gpsimd.tensor_tensor(std[:, :], moments[:, :, 1], half[:, :], ALU.pow).then_inc(std_ready, 1)

            def out_deviation(s):
                pool.wait_ge(out_var_ready, s.done_batch(2, 2))
                nc.gpsimd.tensor_tensor(out_inv[:, s.parity, :], out_var[:, :], neg_half[:, :],
                                        ALU.pow).then_inc(out_inv_ready, 1)

            def split_hl(s, i):
                pool.wait_ge(hl_hi_ready, s.done(NS, i + 1))
                nc.gpsimd.tensor_tensor(hl["lo"][:, s.parity, i, 0:H], hl_full[:, i, :],
                                        hl["hi"][:, s.parity, i, 0:H].bitcast(F32),
                                        ALU.subtract).then_inc(hl_lo_ready, 1)

            def make_mask(s):
                m, a, at = mask[:, s.parity], adj_stage[:, s.parity], adj_t[:, s.parity]
                pool.wait_ge(adj_t_ready, s.done_batch(1, 1))
                pool.wait_ge(masked_ready, s.done(NS, -NS))
                diagonal = a.rearrange("p n (m q) -> p (n m) q", q=P)[:, 0::NS + 1, :]
                nc.gpsimd.tensor_tensor(m[:, :, 0:P], diagonal, later[:, :, :], ALU.mult)
                nc.gpsimd.tensor_tensor(m[:, :, 2 * P:3 * P], at[:, :, 0:P], not_later[:, :, :], ALU.mult)
                nc.gpsimd.tensor_copy(m[:, 0, P:2 * P], a[:, 0, P:2 * P])
                nc.gpsimd.tensor_copy(m[:, 1, P:2 * P], at[:, 1, P:2 * P]).then_inc(mask_ready, 1)

            def slot(s, at_start, at_end):
                prev, nxt = s.shift(-1), s.shift(1)
                if not at_start:
                    deviation(prev)
                if not at_end and nxt.layer == 0:
                    make_mask(nxt)
                for i in range(NS):
                    split_hl(s, i)
                if not at_start and prev.layer == 1:
                    out_deviation(prev)

            def first():
                nc.gpsimd.memset(half[:, :], 0.5)
                nc.gpsimd.memset(neg_half[:, :], -0.5)
                nc.gpsimd.memset(ident[:, :], 1.0).then_inc(ident_filled, 1)
                pool.wait_ge(ident_filled, 1)
                nc.gpsimd.affine_select(out=ident[:, :], in_=ident[:, :], pattern=[[-1, P]], compare_op=ALU.is_equal,
                                        fill=0.0, base=0, channel_multiplier=1).then_inc(consts_ready, 1)
                nc.gpsimd.memset(later[:, :, :], 1.0).then_inc(ident_filled, 1)
                nc.gpsimd.memset(not_later[:, :, :], 1.0).then_inc(ident_filled, 1)
                pool.wait_ge(ident_filled, 3)
                for j in range(NS):
                    nc.gpsimd.affine_select(out=later[:, j, :], in_=later[:, j, :], pattern=[[1, P]],
                                            compare_op=ALU.is_gt, fill=0.0, base=0,
                                            channel_multiplier=-1).then_inc(consts_ready, 1)
                    nc.gpsimd.affine_select(out=not_later[:, j, :], in_=not_later[:, j, :], pattern=[[-1, P]],
                                            compare_op=ALU.is_ge, fill=0.0, base=0,
                                            channel_multiplier=1).then_inc(consts_ready, 1)
                pool.wait_ge(consts_ready, 1 + 2 * NS)
                make_mask(Slot(0, 0))

            def last():
                deviation(LAST)
                out_deviation(LAST)

            run_slots(pool, slot, first, last)


_INS = ["x", "adj", "L0_gnn_W_left", "L0_gnn_W_right", "L0_gnn_W_lin", "L0_gnn_b_lin", "L0_gnn_ln_a", "L0_gnn_ln_b"]


def kernel(**inputs):
    import numpy as _np
    import concourse.bacc as _bacc
    from concourse import mybir as _mybir
    from concourse.bass_utils import run_bass_kernel_spmd as _run

    nc = _bacc.Bacc("TRN2", target_bir_lowering=False, num_devices=1)
    arrays, args = {}, []
    for name in _INS:
        a = _np.ascontiguousarray(inputs[name])
        arrays[f"in_{name}"] = a
        args.append(nc.dram_tensor(f"in_{name}", a.shape, _mybir.dt.from_np(a.dtype), kind="ExternalInput").ap())
    out = nc.dram_tensor("out_0", inputs["x"].shape, _mybir.dt.float32, kind="ExternalOutput").ap()
    build(nc, *args, out)
    r = _run(nc, [arrays], core_ids=[0])
    return r.results[0]["out_0"]
```

```python
from contextlib import ExitStack

import concourse.bass as bass
from concourse import mybir

F32 = mybir.dt.float32
F32R = mybir.dt.float32r
ALU = mybir.AluOpType
ACT = mybir.ActivationFunctionType

P = 128
PAIR = 2
PHASES = 4
LN_EPS = 1e-3
SUM_EPS = 1e-10
OUT_EPS = 1e-5
PASSES = (("hi", "hi"), ("lo", "hi"), ("hi", "lo"))


class Slot:

    def __init__(self, pair, phase):
        self.pair, self.phase = pair, phase
        self.parity = phase % PAIR
        self.layer = phase // PAIR
        self.batch = pair * PAIR + self.parity

    @staticmethod
    def count(n):
        if isinstance(n, int):
            return max(n, 0)
        assert n.min_val > 0
        return n

    def shift(self, d):
        return Slot(self.pair + (self.phase + d) // PHASES, (self.phase + d) % PHASES)

    def done(self, per_slot, k):
        n = self.pair * (PHASES * per_slot) + (self.phase * per_slot + k)
        return self.count(n)

    def done_batch(self, per_batch, k):
        n = self.pair * (PAIR * per_batch) + (self.parity * per_batch + k)
        return self.count(n)

    def done_own(self, per, k):
        n = self.pair * per + k
        return self.count(n)


def build(nc, x, adj, w_left, w_right, w_lin, b_lin, ln_a, ln_b, out):
    B, S, H = x.shape
    L = w_left.shape[0]
    NS, NH = S // P, H // P
    assert S == 2 * P and H == 3 * P and L == 2 and B % PAIR == 0
    PAIRS = B // PAIR
    TEMPER = float(H) ** 0.5
    SCORES = 3 * P
    HL = H + 2
    DDOF = (H / (H - 1.0)) ** 0.5

    with ExitStack() as ctx:
        def sb(name, shape, dt=F32):
            return ctx.enter_context(nc.sbuf_tensor(name, shape, dt))

        def bank(name, shape):
            return ctx.enter_context(nc.psum_tensor(name, shape, F32))

        def sem(name):
            return ctx.enter_context(nc.semaphore(name))

        def parts(name, shape):
            return {"hi": sb(name + "_hi", shape, F32R), "lo": sb(name + "_lo", shape, F32R)}

        wr = parts("wr", [P, L, NH, H])
        wl = parts("wl", [P, L, NH, H])
        wt = parts("wt", [P, L, NH, H])
        w_stage = sb("w_stage", [P, 3, NH, H])
        b_row = sb("b_row", [P, L, H])
        a_row = sb("a_row", [P, H])
        c_row = sb("c_row", [P, H])
        a_col = sb("a_col", [P, NH])
        c_col = sb("c_col", [P, NH])
        ident = sb("ident", [P, P])
        later = sb("later", [P, NS, P])
        not_later = sb("not_later", [P, NS, P])
        half = sb("half", [P, NS])
        neg_half = sb("neg_half", [P, NS])
        x_stage = sb("x_stage", [P, PAIR, NS, H])
        x_res = sb("x_res", [P, PAIR, NS, H])
        adj_stage = sb("adj_stage", [P, PAIR, NS, S])
        mask = sb("mask", [P, PAIR, NS, SCORES])
        adj_t = sb("adj_t", [P, PAIR, NS, S])
        ht = parts("ht", [P, PAIR, NH, S])
        hl = parts("hl", [P, PAIR, NS, HL])
        y = sb("y", [P, PAIR, NS, H])
        h_full = sb("h_full", [P, NH, S])
        g = parts("g", [P, NH, 2 * S])
        hl_full = sb("hl_full", [P, NS, H])
        masked = sb("masked", [P, NS, SCORES])
        expd = sb("expd", [P, NS, S])
        p_full = sb("p_full", [P, NS, S])
        pt = parts("pt", [P, NS, S])
        z = sb("z", [P, NS, H])
        stats = sb("stats", [P, NS, 6])
        moments = sb("moments", [P, NS, 2])
        sum_eps = sb("sum_eps", [P, NS])
        std = sb("std", [P, NS])
        denom = sb("denom", [P, NS])
        inv_std = sb("inv_std", [P, NS])
        shift = sb("shift", [P, NS])
        out_stats = sb("out_stats", [P, NS, 6])
        out_moments = sb("out_moments", [P, NS, 2])
        out_var = sb("out_var", [P, PAIR, NS])
        out_inv = sb("out_inv", [P, PAIR, NS])
        out_mean = sb("out_mean", [P, PAIR, NS])
        out_shift = sb("out_shift", [P, PAIR, NS])

        proj = [bank(f"proj{c}", [P, 2 * S]) for c in range(NH)]
        score = [bank(f"score{j}", [P, 2 * S]) for j in range(NS)]
        ctx_ps = bank("ctx_ps", [P, NS, 2 * S])
        tr = bank("tr", [P, 2 * S])
        tr_bank = [tr[:, 0:S], ctx_ps[:, 0, 0:S], ctx_ps[:, 1, 0:S]]
        lin_bank = [[score[1][:, 0:H], ctx_ps[:, 0, 0:H], ctx_ps[:, 1, 0:H]], [proj[c][:, 0:H] for c in range(NH)]]

        w_loaded = [[sem(f"w{l}{n}_loaded") for n in ("right", "left", "lin")] for l in range(L)]
        rows_loaded = sem("rows_loaded")
        x_loaded = [sem(f"x_loaded{p}") for p in range(PAIR)]
        adj_loaded = [sem(f"adj_loaded{p}") for p in range(PAIR)]
        x_copied = [sem(f"x_copied{p}") for p in range(PAIR)]
        stored = [sem(f"stored{p}") for p in range(PAIR)]
        consts_ready = sem("consts_ready")
        ident_filled = sem("ident_filled")
        ones_ready = sem("ones_ready")
        wt_done = sem("wt_done")
        wt_hi_ready = sem("wt_hi_ready")
        wt_lo_ready = sem("wt_lo_ready")
        w_hi_ready = sem("w_hi_ready")
        w_lo_ready = sem("w_lo_ready")
        transposed = sem("transposed")
        h_full_ready = sem("h_full_ready")
        ht_hi_ready = sem("ht_hi_ready")
        ht_lo_ready = sem("ht_lo_ready")
        g_done = sem("g_done")
        g_hi_ready = sem("g_hi_ready")
        g_lo_ready = sem("g_lo_ready")
        hl_done = sem("hl_done")
        hl_full_ready = sem("hl_full_ready")
        hl_hi_ready = sem("hl_hi_ready")
        hl_lo_ready = sem("hl_lo_ready")
        score_done = sem("score_done")
        masked_ready = sem("masked_ready")
        summed_ready = sem("summed_ready")
        exp_ready = sem("exp_ready")
        p_full_ready = sem("p_full_ready")
        p_hi_ready = sem("p_hi_ready")
        p_lo_ready = sem("p_lo_ready")
        ctx_done = sem("ctx_done")
        stats_ready = sem("stats_ready")
        moments_ready = sem("moments_ready")
        std_ready = sem("std_ready")
        denom_ready = sem("denom_ready")
        inv_ready = sem("inv_ready")
        shift_ready = sem("shift_ready")
        adj_done = sem("adj_done")
        adj_t_ready = sem("adj_t_ready")
        mask_ready = sem("mask_ready")
        z_ready = sem("z_ready")
        centred_ready = sem("centred_ready")
        scaled_ready = sem("scaled_ready")
        resid_ready = sem("resid_ready")
        out_stats_ready = sem("out_stats_ready")
        out_moments_ready = sem("out_moments_ready")
        out_var_ready = sem("out_var_ready")
        out_inv_ready = sem("out_inv_ready")
        out_shift_ready = sem("out_shift_ready")
        out_ready = sem("out_ready")

        def element(dram, b):
            size = dram.shape[1] * dram.shape[2]
            flat = dram.rearrange("b s h -> (b s h)")[bass.ds(b * size, size)]
            return flat.rearrange("(n p h) -> p n h", p=P, h=dram.shape[2])

        def ahead(eng, dram, b, *counts):
            for value in (b * (dram.shape[1] * dram.shape[2] * 4), *counts):
                if not isinstance(value, int):
                    eng.to_reg(value)

        block = ctx.enter_context(nc.Block())

        def run_slots(eng, slot, first, last):
            first()
            for phase in (0, 1):
                slot(Slot(0, phase), at_start=(phase == 0), at_end=False)
            with eng.Fori(0, PAIRS - 1) as pair:
                for phase in (2, 3):
                    slot(Slot(pair, phase), at_start=False, at_end=False)
                for phase in (0, 1):
                    slot(Slot(pair + 1, phase), at_start=False, at_end=False)
            for phase in (2, 3):
                slot(Slot(PAIRS - 1, phase), at_start=False, at_end=(phase == 3))
            last()

        LAST = Slot(PAIRS - 1, PHASES - 1)

        @block.sync
        def _(sp):
            def load_x(b):
                sp.dma_start(x_stage[:, b], element(x, b)).then_inc(x_loaded[b], 16)

            def load_adj(b):
                sp.dma_start(adj_stage[:, b], element(adj, b)).then_inc(adj_loaded[b], 16)

            def load_w(l, n, w):
                sp.dma_start(w_stage[:, n], w[l].rearrange("(k p) h -> p k h", p=P)).then_inc(w_loaded[l][n], 16)

            def first():
                load_x(0)
                load_w(0, 1, w_left)
                load_w(0, 2, w_lin)
                load_adj(0)
                load_x(1)
                load_adj(1)
                for n, w in enumerate((w_right, w_left)):
                    sp.wait_ge(w_lo_ready, n + 1)
                    load_w(1, n, w)
                sp.wait_ge(wt_done, NH)
                load_w(1, 2, w_lin)

            def store(s):
                ahead(sp, out, s.batch, s.done_batch(NS, NS))
                sp.wait_ge(out_ready, s.done_batch(NS, NS))
                sp.dma_start(element(out, s.batch), y[:, s.parity]).then_inc(stored[s.parity], 16)

            def put_by(s, more):
                p = s.parity
                if more:
                    ahead(sp, x, s.batch + PAIR, s.done_own(16, 0), s.done_own(16, 16), s.done(NH, NH),
                          s.done_batch(1, 1))
                    ahead(sp, adj, s.batch + PAIR)
                sp.wait_ge(x_loaded[p], s.done_own(16, 16))
                sp.wait_ge(stored[p], s.done_own(16, 0))
                sp.dma_start(x_res[:, p], x_stage[:, p]).then_inc(x_copied[p], 16)
                if more:
                    sp.wait_ge(x_copied[p], s.done_own(16, 16))
                    sp.wait_ge(transposed, s.done(NH, NH))
                    sp.wait_ge(mask_ready, s.done_batch(1, 1))
                    sp.dma_start(x_stage[:, p], element(x, s.batch + PAIR)).then_inc(x_loaded[p], 16)
                    sp.dma_start(adj_stage[:, p], element(adj, s.batch + PAIR)).then_inc(adj_loaded[p], 16)

            first()
            for phase in (0, 1):
                put_by(Slot(0, phase), True)
            with sp.Fori(0, PAIRS - 2) as pair:
                for phase in (0, 1):
                    store(Slot(pair, phase))
                    put_by(Slot(pair + 1, phase), True)
            for phase in (0, 1):
                store(Slot(PAIRS - 2, phase))
                put_by(Slot(PAIRS - 1, phase), False)
            for phase in (0, 1):
                store(Slot(PAIRS - 1, phase))
            for p in range(PAIR):
                sp.wait_ge(stored[p], 16 * PAIRS)

        @block.tensor
        def _(pe):
            def transpose_lin(l):
                pe.wait_ge(w_loaded[l][2], 16)
                for k in range(NH):
                    if l == 0:
                        pe.wait_ge(ht_lo_ready, k + 1)
                    elif k < NS:
                        pe.wait_ge(hl_full_ready, k + 1)
                    else:
                        pe.wait_ge(g_lo_ready, k + 1)
                    for o in range(NH):
                        last = nc.tensor.transpose(lin_bank[l][k][:, o * P:(o + 1) * P],
                                                   w_stage[:, 2, o, k * P:(k + 1) * P], ident[:, :])
                    last.then_inc(wt_done, 1)

            def transpose_h(s):
                if s.layer == 0:
                    pe.wait_ge(x_loaded[s.parity], s.done_own(16, 16))
                    pe.wait_ge(centred_ready, s.done_batch(NS, -NS))
                    src = x_stage[:, s.parity]
                else:
                    pe.wait_ge(z_ready, s.done_batch(NS, NS))
                    src = z
                for k in range(NH):
                    if k == 0:
                        pe.wait_ge(ht_lo_ready, s.done(NH, 1 - NH))
                    for i in range(NS):
                        last = nc.tensor.transpose(tr_bank[k][:, i * P:(i + 1) * P],
                                                   src[:, i, k * P:(k + 1) * P], ident[:, :])
                    last.then_inc(transposed, 1)

            def project(s, c):
                if c < NS:
                    pe.wait_ge(hl_full_ready, s.done(NS, c + 1 - NS))
                if s.phase == 1 and isinstance(s.pair, int):
                    pe.wait_ge(wt_lo_ready, NH + c + 1)
                for w, at in ((wr, 0), (wl, S)):
                    for k in range(NH):
                        for n, (a, b) in enumerate(PASSES):
                            if c == 0 and at == 0 and n == 0:
                                pe.wait_ge(ht_hi_ready, s.done(NH, k + 1))
                            if c == 0 and k == 0 and n < 2:
                                if a == "hi":
                                    pe.wait_ge(w_hi_ready, 2 * s.layer + at // S + 1)
                                else:
                                    pe.wait_ge(w_lo_ready, 2 * s.layer + at // S + 1)
                            if c == 0 and at == 0 and n == 2:
                                pe.wait_ge(ht_lo_ready, s.done(NH, k + 1))
                            last = nc.tensor.matmul(proj[c][:, at:at + S],
                                                    w[a][:, s.layer, k, c * P:(c + 1) * P],
                                                    ht[b][:, s.parity, k, :],
                                                    start=(k == 0 and n == 0), stop=(k == NH - 1 and n == 2))
                last.then_inc(g_done, 1)

            def linear(s, i):
                if i == 0:
                    pe.wait_ge(wt_lo_ready, NH * (s.layer + 1))
                pe.wait_ge(g_lo_ready, s.done(NH, i + 1))
                for k in range(NH):
                    for n, (a, b) in enumerate(PASSES):
                        last = nc.tensor.matmul(proj[i][:, 0:H], ht[a][:, s.parity, k, i * P:(i + 1) * P],
                                                wt[b][:, s.layer, k, :],
                                                start=(k == 0 and n == 0), stop=(k == NH - 1 and n == 2))
                last.then_inc(hl_done, 1)

            def scores(s, j):
                if j == 0:
                    pe.wait_ge(g_lo_ready, s.done(NH, NH))
                    pe.wait_ge(adj_t_ready, s.done_batch(1, 1))
                pe.wait_ge(masked_ready, s.done(NS, j + 1 - NS))
                for k in range(NH):
                    for n, (a, b) in enumerate(PASSES):
                        last = nc.tensor.matmul(score[j][:, 0:SCORES], ht[a][:, s.parity, k, j * P:(j + 1) * P],
                                                g[b][:, k, j * P:j * P + SCORES],
                                                start=(k == 0 and n == 0), stop=(k == NH - 1 and n == 2))
                last.then_inc(score_done, 1)

            def context(s, i):
                if i == 0:
                    pe.wait_ge(p_lo_ready, s.done(NS, NS))
                    pe.wait_ge(hl_lo_ready, s.done(NS, NS))
                    if s is not LAST:
                        pe.wait_ge(ht_lo_ready, s.done(NH, 2 * NH))
                for j in range(NS):
                    q = i if j == 0 else 1 - i
                    for n, (a, b) in enumerate(PASSES):
                        wide = HL if b == "hi" else H
                        last = nc.tensor.matmul(ctx_ps[:, i, 0:wide], pt[a][:, j, q * P:(q + 1) * P],
                                                hl[b][:, s.parity, j, 0:wide],
                                                start=(j == 0 and n == 0), stop=(j == NS - 1 and n == 2))
                last.then_inc(ctx_done, 1)

            def transpose_adj(s):
                pe.wait_ge(adj_loaded[s.parity], s.done_own(16, 16))
                if isinstance(s.pair, int) and s.pair == 0:
                    pe.wait_ge(adj_t_ready, s.done_batch(1, 0))
                else:
                    pe.wait_ge(masked_ready, s.done(NS, -NS - 1))
                for j in range(NS):
                    for n in range(NS):
                        i = n if j == 0 else 1 - n
                        last = nc.tensor.transpose(score[0][:, (2 * j + n) * P:(2 * j + n + 1) * P],
                                                   adj_stage[:, s.parity, i, j * P:(j + 1) * P], ident[:, :])
                last.then_inc(adj_done, 1)

            def slot(s, at_start, at_end):
                prev, nxt = s.shift(-1), s.shift(1)
                project(s, 0)
                project(s, 1)
                if at_start:
                    transpose_lin(0)
                    transpose_adj(s)
                if not at_start:
                    context(prev, 0)
                    context(prev, 1)
                if not at_end and nxt.layer == 0:
                    transpose_adj(nxt)
                project(s, 2)
                for i in range(NS):
                    linear(s, i)
                if not at_end:
                    transpose_h(nxt)
                scores(s, 0)
                scores(s, 1)
                if at_start:
                    transpose_lin(1)

            def first():
                pe.wait_ge(consts_ready, 1)
                pe.wait_ge(ones_ready, PAIR * NS)
                transpose_h(Slot(0, 0))

            def last():
                for i in range(NS):
                    context(LAST, i)

            run_slots(pe, slot, first, last)

        @block.scalar
        def _(act):
            def take_w(l):
                for n, w in enumerate((wr, wl)):
                    act.wait_ge(w_loaded[l][n], 16)
                    nc.scalar.copy(w["hi"][:, l], w_stage[:, n]).then_inc(w_hi_ready, 1)

            def take_lin(l):
                for k in range(NH):
                    act.wait_ge(wt_done, NH * l + k + 1)
                    nc.scalar.copy(wt["hi"][:, l, k, :], lin_bank[l][k]).then_inc(wt_hi_ready, 1)

            def take_h(s):
                act.wait_ge(score_done, s.done(NS, -NS))
                for k in range(NH):
                    act.wait_ge(transposed, s.done(NH, k + 1))
                    if s.layer == 0:
                        nc.scalar.copy(ht["hi"][:, s.parity, k, :], tr_bank[k]).then_inc(ht_hi_ready, 1)
                    else:
                        nc.scalar.activation(h_full[:, k, :], tr_bank[k], ACT.Relu, bias=c_col[:, k:k + 1],
                                             scale=a_col[:, k:k + 1]).then_inc(h_full_ready, 1)

            def take_g(s, c):
                act.wait_ge(g_done, s.done(NH, c + 1))
                act.wait_ge(score_done, s.done(NS, 0))
                nc.scalar.copy(g["hi"][:, c, :], proj[c][:, :]).then_inc(g_hi_ready, 1)

            def take_hl(s, i):
                act.wait_ge(hl_full_ready, s.done(NS, i + 1))
                act.wait_ge(ctx_done, s.done(NS, -NS))
                nc.scalar.copy(hl["hi"][:, s.parity, i, 0:H], hl_full[:, i, :]).then_inc(hl_hi_ready, 1)

            def exponent(s, j):
                act.wait_ge(summed_ready, s.done(NS, j + 1))
                act.wait_ge(p_full_ready, s.done(NS, j + 1 - NS))
                nc.scalar.activation(expd[:, j, :], masked[:, j, 0:S], ACT.Exp,
                                     scale=1.0 / TEMPER).then_inc(exp_ready, 1)

            def take_p(s, j):
                act.wait_ge(p_full_ready, s.done(NS, j + 1))
                act.wait_ge(ctx_done, s.done(NS, 0))
                nc.scalar.copy(pt["hi"][:, j, :], p_full[:, j, :]).then_inc(p_hi_ready, 1)

            def normalise(s):
                act.wait_ge(shift_ready, s.done(1, 1))
                act.wait_ge(transposed, s.done(NH, 2 * NH))
                for i in range(NS):
                    nc.scalar.activation(z[:, i, :], ctx_ps[:, i, 0:H], ACT.Identity, bias=shift[:, i:i + 1],
                                         scale=inv_std[:, i:i + 1]).then_inc(z_ready, 1)

            def finish(s):
                act.wait_ge(out_shift_ready, s.done_batch(1, 1))
                for i in range(NS):
                    nc.scalar.activation(y[:, s.parity, i, :], y[:, s.parity, i, :], ACT.Identity,
                                         bias=out_shift[:, s.parity, i:i + 1],
                                         scale=out_inv[:, s.parity, i:i + 1]).then_inc(out_ready, 1)

            def take_adj(s):
                act.wait_ge(adj_done, s.done_batch(1, 1))
                act.wait_ge(p_full_ready, s.done(NS, -NS))
                nc.scalar.copy(adj_t[:, s.parity],
                               score[0][:, :].rearrange("p (j q) -> p j q", j=NS)).then_inc(adj_t_ready, 1)

            def slot(s, at_start, at_end):
                prev, before, nxt = s.shift(-1), s.shift(-2), s.shift(1)
                if not at_start:
                    exponent(prev, 1)
                    take_p(prev, 0)
                    take_p(prev, 1)
                take_g(s, 0)
                if at_start:
                    take_lin(0)
                take_g(s, 1)
                if not at_end and nxt.layer == 0:
                    take_adj(nxt)
                if not at_start and prev.layer == 0:
                    normalise(prev)
                take_g(s, 2)
                if before.layer == 1 and not (isinstance(s.pair, int) and s.pair == 0):
                    finish(before)
                for i in range(NS):
                    take_hl(s, i)
                if not at_end:
                    take_h(nxt)
                exponent(s, 0)
                if at_start:
                    take_lin(1)
                    take_w(1)

            def first():
                act.dma_start(w_stage[:, 0], w_right[0].rearrange("(k p) h -> p k h", p=P)).then_inc(w_loaded[0][0], 16)
                act.dma_start(a_col[:, :], ln_a[0].rearrange("(k p) -> p k", p=P),
                              allow_slow_non_contiguous=True).then_inc(rows_loaded, 16)
                act.dma_start(c_col[:, :], ln_b[0].rearrange("(k p) -> p k", p=P),
                              allow_slow_non_contiguous=True).then_inc(rows_loaded, 16)
                for l in range(L):
                    act.dma_start(b_row[:, l, :], b_lin[l].partition_broadcast(P)).then_inc(rows_loaded, 16)
                act.dma_start(a_row[:, :], ln_a[1].partition_broadcast(P)).then_inc(rows_loaded, 16)
                act.dma_start(c_row[:, :], ln_b[1].partition_broadcast(P)).then_inc(rows_loaded, 16)
                take_h(Slot(0, 0))
                take_w(0)
                take_adj(Slot(0, 0))
                act.wait_ge(rows_loaded, 6 * 16)

            def last():
                exponent(LAST, 1)
                take_p(LAST, 0)
                take_p(LAST, 1)
                finish(LAST.shift(-1))
                finish(LAST)

            run_slots(act, slot, first, last)

        @block.vector
        def _(dve):
            def split_lin(l):
                for k in range(NH):
                    dve.wait_ge(wt_hi_ready, NH * l + k + 1)
                    nc.vector.tensor_tensor(wt["lo"][:, l, k, :], lin_bank[l][k], wt["hi"][:, l, k, :].bitcast(F32),
                                            ALU.subtract).then_inc(wt_lo_ready, 1)

            def split_h(s):
                for k in range(NH):
                    hi, lo = (ht[a][:, s.parity, k, :] for a in ("hi", "lo"))
                    if s.layer == 1:
                        dve.wait_ge(h_full_ready, s.done_batch(NH, k + 1))
                        nc.vector.tensor_copy(hi, h_full[:, k, :]).then_inc(ht_hi_ready, 1)
                    dve.wait_ge(ht_hi_ready, s.done(NH, k + 1))
                    nc.vector.tensor_tensor(lo, h_full[:, k, :] if s.layer else tr_bank[k], hi.bitcast(F32),
                                            ALU.subtract).then_inc(ht_lo_ready, 1)

            def split_g(s, c):
                dve.wait_ge(g_hi_ready, s.done(NH, c + 1))
                nc.vector.tensor_tensor(g["lo"][:, c, :], proj[c][:, :], g["hi"][:, c, :].bitcast(F32),
                                        ALU.subtract).then_inc(g_lo_ready, 1)

            def add_bias(s, i):
                dve.wait_ge(hl_done, s.done(NS, i + 1))
                dve.wait_ge(hl_lo_ready, s.done(NS, i + 1 - NS))
                nc.vector.tensor_tensor(hl_full[:, i, :], proj[i][:, 0:H], b_row[:, s.layer, :],
                                        ALU.add).then_inc(hl_full_ready, 1)

            def mask_scores(s, j):
                dve.wait_ge(score_done, s.done(NS, j + 1))
                dve.wait_ge(mask_ready, s.done_batch(1, 1))
                dve.wait_ge(exp_ready, s.done(NS, j + 1 - NS))
                nc.vector.tensor_tensor(masked[:, j, :], score[j][:, 0:SCORES], mask[:, s.parity, j, :],
                                        ALU.mult).then_inc(masked_ready, 1)
                dve.wait_ge(masked_ready, s.done(NS, j + 1))
                nc.vector.tensor_tensor(masked[:, j, 0:P], masked[:, j, 0:P], masked[:, j, 2 * P:3 * P],
                                        ALU.add).then_inc(summed_ready, 1)

            def weigh(s, j):
                dve.wait_ge(exp_ready, s.done(NS, j + 1))
                nc.vector.tensor_tensor(p_full[:, j, :], expd[:, j, :], adj_t[:, s.parity, j, :],
                                        ALU.mult).then_inc(p_full_ready, 1)

            def split_p(s, j):
                dve.wait_ge(p_hi_ready, s.done(NS, j + 1))
                nc.vector.tensor_tensor(pt["lo"][:, j, :], p_full[:, j, :], pt["hi"][:, j, :].bitcast(F32),
                                        ALU.subtract).then_inc(p_lo_ready, 1)

            def norm_scalars(s):
                for i in range(NS):
                    dve.wait_ge(ctx_done, s.done(NS, i + 1))
                    nc.vector.bn_stats(stats[:, i, :], ctx_ps[:, i, 0:H]).then_inc(stats_ready, 1)
                dve.wait_ge(stats_ready, s.done(NS, NS))
                nc.vector.tensor_scalar(sum_eps[:, :], ctx_ps[:, :, H], LN_EPS, LN_EPS * SUM_EPS, ALU.mult,
                                        ALU.add).then_inc(moments_ready, 1)
                for i in range(NS):
                    nc.vector.bn_aggr(moments[:, i, :], stats[:, i, :]).then_inc(moments_ready, 1)
                dve.wait_ge(std_ready, s.done(1, 1))
                dve.wait_ge(moments_ready, s.done(3, 3))
                nc.vector.scalar_tensor_tensor(denom[:, :], std[:, :], DDOF, sum_eps[:, :], ALU.mult,
                                               ALU.add).then_inc(denom_ready, 1)
                dve.wait_ge(denom_ready, s.done(1, 1))
                nc.vector.reciprocal(inv_std[:, :], denom[:, :]).then_inc(inv_ready, 1)
                dve.wait_ge(inv_ready, s.done(1, 1))
                if s.layer == 0:
                    nc.vector.scalar_tensor_tensor(shift[:, :], moments[:, :, 0], -1.0, inv_std[:, :], ALU.mult,
                                                   ALU.mult).then_inc(shift_ready, 1)
                else:
                    nc.vector.scalar_tensor_tensor(shift[:, :], moments[:, :, 0], -1.0, inv_std[:, :], ALU.mult,
                                                   ALU.mult).then_inc(shift_ready, 1)

            def centre(s):
                dve.wait_ge(x_copied[s.parity], s.done_own(16, 16))
                for i in range(NS):
                    nc.vector.scalar_tensor_tensor(y[:, s.parity, i, :], ctx_ps[:, i, 0:H], moments[:, i, 0:1],
                                                   a_row[:, :], ALU.subtract, ALU.mult).then_inc(centred_ready, 1)

            def scale(s, i):
                yi = y[:, s.parity, i, :]
                dve.wait_ge(centred_ready, s.done_batch(NS, i + 1))
                nc.vector.scalar_tensor_tensor(yi, yi, inv_std[:, i:i + 1], c_row[:, :], ALU.mult,
                                               ALU.add).then_inc(scaled_ready, 1)

            def add_residual(s, i):
                yi = y[:, s.parity, i, :]
                dve.wait_ge(scaled_ready, s.done_batch(NS, i + 1))
                nc.vector.scalar_tensor_tensor(yi, yi, 0.0, x_res[:, s.parity, i, :], ALU.max,
                                               ALU.add).then_inc(resid_ready, 1)

            def measure(s, i):
                dve.wait_ge(resid_ready, s.done_batch(NS, i + 1))
                nc.vector.bn_stats(out_stats[:, i, :], y[:, s.parity, i, :]).then_inc(out_stats_ready, 1)

            def out_variance(s):
                for i in range(NS):
                    nc.vector.bn_aggr(out_moments[:, i, :], out_stats[:, i, :]).then_inc(out_moments_ready, 1)
                dve.wait_ge(out_moments_ready, s.done_batch(NS, NS))
                nc.vector.tensor_scalar(out_var[:, s.parity, :], out_moments[:, :, 1], OUT_EPS, None,
                                        ALU.add).then_inc(out_var_ready, 1)
                nc.vector.tensor_copy(out_mean[:, s.parity, :], out_moments[:, :, 0]).then_inc(out_var_ready, 1)

            def out_scalars(s):
                dve.wait_ge(out_inv_ready, s.done_batch(1, 1))
                nc.vector.scalar_tensor_tensor(out_shift[:, s.parity, :], out_mean[:, s.parity, :], -1.0,
                                               out_inv[:, s.parity, :], ALU.mult,
                                               ALU.mult).then_inc(out_shift_ready, 1)

            def slot(s, at_start, at_end):
                prev, before, nxt = s.shift(-1), s.shift(-2), s.shift(1)
                output = not at_start and prev.layer == 1
                output_before = before.layer == 1 and not (isinstance(s.pair, int) and s.pair == 0)
                if not at_start:
                    mask_scores(prev, 1)
                    weigh(prev, 0)
                    weigh(prev, 1)
                    split_p(prev, 0)
                    split_p(prev, 1)
                if output_before:
                    measure(before, 0)
                    measure(before, 1)
                    dve.wait_ge(out_stats_ready, before.done_batch(NS, NS))
                split_g(s, 0)
                if output_before:
                    out_variance(before)
                if at_start:
                    split_lin(0)
                split_g(s, 1)
                if not at_start:
                    norm_scalars(prev)
                    if output:
                        centre(prev)
                split_g(s, 2)
                if output_before:
                    out_scalars(before)
                if output:
                    scale(prev, 0)
                    scale(prev, 1)
                add_bias(s, 0)
                if output:
                    add_residual(prev, 0)
                add_bias(s, 1)
                if output:
                    add_residual(prev, 1)
                if not at_end:
                    split_h(nxt)
                mask_scores(s, 0)
                if at_start:
                    split_lin(1)

            def first():
                ones = [hl["hi"][:, p, i, H:HL].bitcast(F32) for p in range(PAIR) for i in range(NS)]
                for t in ones:
                    nc.vector.memset(t, 1.0).then_inc(ones_ready, 1)
                split_h(Slot(0, 0))
                for n, w in enumerate((wr, wl)):
                    dve.wait_ge(w_hi_ready, n + 1)
                    nc.vector.tensor_tensor(w["lo"][:, 0], w_stage[:, n], w["hi"][:, 0].bitcast(F32),
                                            ALU.subtract).then_inc(w_lo_ready, 1)
                dve.wait_ge(rows_loaded, 6 * 16)

            def last():
                before = LAST.shift(-1)
                mask_scores(LAST, 1)
                weigh(LAST, 0)
                weigh(LAST, 1)
                split_p(LAST, 0)
                split_p(LAST, 1)
                for i in range(NS):
                    measure(before, i)
                dve.wait_ge(out_stats_ready, before.done_batch(NS, NS))
                out_variance(before)
                norm_scalars(LAST)
                out_scalars(before)
                centre(LAST)
                for i in range(NS):
                    scale(LAST, i)
                for i in range(NS):
                    add_residual(LAST, i)
                for i in range(NS):
                    measure(LAST, i)
                dve.wait_ge(out_stats_ready, LAST.done_batch(NS, NS))
                out_variance(LAST)
                out_scalars(LAST)

            run_slots(dve, slot, first, last)

        @block.gpsimd
        def _(pool):
            def deviation(s):
                pool.wait_ge(moments_ready, s.done(3, 3))
                pool.wait_ge(denom_ready, s.done(1, 0))
                nc.gpsimd.tensor_tensor(std[:, :], moments[:, :, 1], half[:, :], ALU.pow).then_inc(std_ready, 1)

            def out_deviation(s):
                pool.wait_ge(out_var_ready, s.done_batch(2, 2))
                nc.gpsimd.tensor_tensor(out_inv[:, s.parity, :], out_var[:, s.parity, :], neg_half[:, :],
                                        ALU.pow).then_inc(out_inv_ready, 1)

            def split_hl(s, i):
                pool.wait_ge(hl_hi_ready, s.done(NS, i + 1))
                nc.gpsimd.tensor_tensor(hl["lo"][:, s.parity, i, 0:H], hl_full[:, i, :],
                                        hl["hi"][:, s.parity, i, 0:H].bitcast(F32),
                                        ALU.subtract).then_inc(hl_lo_ready, 1)

            def make_mask(s):
                m, a, at = mask[:, s.parity], adj_stage[:, s.parity], adj_t[:, s.parity]
                pool.wait_ge(adj_t_ready, s.done_batch(1, 1))
                pool.wait_ge(masked_ready, s.done(NS, -NS))
                diagonal = a.rearrange("p n (m q) -> p (n m) q", q=P)[:, 0::NS + 1, :]
                nc.gpsimd.tensor_tensor(m[:, :, 0:P], diagonal, later[:, :, :], ALU.mult)
                nc.gpsimd.tensor_tensor(m[:, :, 2 * P:3 * P], at[:, :, 0:P], not_later[:, :, :], ALU.mult)
                nc.gpsimd.tensor_copy(m[:, 0, P:2 * P], a[:, 0, P:2 * P])
                nc.gpsimd.tensor_copy(m[:, 1, P:2 * P], at[:, 1, P:2 * P]).then_inc(mask_ready, 1)

            def slot(s, at_start, at_end):
                prev, nxt = s.shift(-1), s.shift(1)
                before = s.shift(-2)
                if before.layer == 1 and not (isinstance(s.pair, int) and s.pair == 0):
                    out_deviation(before)
                if not at_start:
                    deviation(prev)
                if not at_end and nxt.layer == 0:
                    make_mask(nxt)
                for i in range(NS):
                    split_hl(s, i)
                if at_start:
                    for n, w in enumerate((wr, wl)):
                        pool.wait_ge(w_hi_ready, 2 + n + 1)
                        nc.gpsimd.tensor_tensor(w["lo"][:, 1], w_stage[:, n], w["hi"][:, 1].bitcast(F32),
                                                ALU.subtract).then_inc(w_lo_ready, 1)

            def first():
                nc.gpsimd.memset(ident[:, :], 1.0).then_inc(ident_filled, 1)
                pool.wait_ge(ident_filled, 1)
                nc.gpsimd.affine_select(out=ident[:, :], in_=ident[:, :], pattern=[[-1, P]], compare_op=ALU.is_equal,
                                        fill=0.0, base=0, channel_multiplier=1).then_inc(consts_ready, 1)
                nc.gpsimd.memset(half[:, :], 0.5)
                nc.gpsimd.memset(neg_half[:, :], -0.5)
                nc.gpsimd.memset(later[:, :, :], 1.0).then_inc(ident_filled, 1)
                nc.gpsimd.memset(not_later[:, :, :], 1.0).then_inc(ident_filled, 1)
                pool.wait_ge(ident_filled, 3)
                for j in range(NS):
                    nc.gpsimd.affine_select(out=later[:, j, :], in_=later[:, j, :], pattern=[[1, P]],
                                            compare_op=ALU.is_gt, fill=0.0, base=0,
                                            channel_multiplier=-1).then_inc(consts_ready, 1)
                    nc.gpsimd.affine_select(out=not_later[:, j, :], in_=not_later[:, j, :], pattern=[[-1, P]],
                                            compare_op=ALU.is_ge, fill=0.0, base=0,
                                            channel_multiplier=1).then_inc(consts_ready, 1)
                pool.wait_ge(consts_ready, 1 + 2 * NS)
                make_mask(Slot(0, 0))

            def last():
                out_deviation(LAST.shift(-1))
                deviation(LAST)
                out_deviation(LAST)

            run_slots(pool, slot, first, last)


_INS = ["x", "adj", "L0_gnn_W_left", "L0_gnn_W_right", "L0_gnn_W_lin", "L0_gnn_b_lin", "L0_gnn_ln_a", "L0_gnn_ln_b"]


def kernel(**inputs):
    import numpy as _np
    import concourse.bacc as _bacc
    from concourse import mybir as _mybir
    from concourse.bass_utils import run_bass_kernel_spmd as _run

    nc = _bacc.Bacc("TRN2", target_bir_lowering=False, num_devices=1)
    arrays, args = {}, []
    for name in _INS:
        a = _np.ascontiguousarray(inputs[name])
        arrays[f"in_{name}"] = a
        args.append(nc.dram_tensor(f"in_{name}", a.shape, _mybir.dt.from_np(a.dtype), kind="ExternalInput").ap())
    out = nc.dram_tensor("out_0", inputs["x"].shape, _mybir.dt.float32, kind="ExternalOutput").ap()
    build(nc, *args, out)
    r = _run(nc, [arrays], core_ids=[0])
    return r.results[0]["out_0"]
```

```python
from contextlib import ExitStack

import concourse.bass as bass
from concourse import mybir

F32 = mybir.dt.float32
F32R = mybir.dt.float32r
ALU = mybir.AluOpType
ACT = mybir.ActivationFunctionType

P = 128
PAIR = 2
PHASES = 4
LN_EPS = 1e-3
SUM_EPS = 1e-10
OUT_EPS = 1e-5
PASSES = (("hi", "hi"), ("lo", "hi"), ("hi", "lo"))


class Slot:

    def __init__(self, pair, phase):
        self.pair, self.phase = pair, phase
        self.parity = phase % PAIR
        self.layer = phase // PAIR
        self.batch = pair * PAIR + self.parity

    @staticmethod
    def count(n):
        if isinstance(n, int):
            return max(n, 0)
        assert n.min_val > 0
        return n

    def shift(self, d):
        return Slot(self.pair + (self.phase + d) // PHASES, (self.phase + d) % PHASES)

    def done(self, per_slot, k):
        n = self.pair * (PHASES * per_slot) + (self.phase * per_slot + k)
        return self.count(n)

    def done_batch(self, per_batch, k):
        n = self.pair * (PAIR * per_batch) + (self.parity * per_batch + k)
        return self.count(n)

    def done_own(self, per, k):
        n = self.pair * per + k
        return self.count(n)


def build(nc, x, adj, w_left, w_right, w_lin, b_lin, ln_a, ln_b, out):
    B, S, H = x.shape
    L = w_left.shape[0]
    NS, NH = S // P, H // P
    assert S == 2 * P and H == 3 * P and L == 2 and B % PAIR == 0
    PAIRS = B // PAIR
    TEMPER = float(H) ** 0.5
    SCORES = 3 * P
    HL = H + 2
    WARM_UP = 28
    TILE = 32
    QUARTERS = P // TILE
    DDOF = (H / (H - 1.0)) ** 0.5

    with ExitStack() as ctx:
        def sb(name, shape, dt=F32):
            return ctx.enter_context(nc.sbuf_tensor(name, shape, dt))

        def bank(name, shape):
            return ctx.enter_context(nc.psum_tensor(name, shape, F32))

        def sem(name):
            return ctx.enter_context(nc.semaphore(name))

        def parts(name, shape):
            return {"hi": sb(name + "_hi", shape, F32R), "lo": sb(name + "_lo", shape, F32R)}

        wr = parts("wr", [P, L, NH, H])
        wl = parts("wl", [P, L, NH, H])
        wt = parts("wt", [P, L, NH, H])
        w_stage = sb("w_stage", [P, 3, NH, H])
        b_row = sb("b_row", [P, L, H])
        a_row = sb("a_row", [P, H])
        c_row = sb("c_row", [P, H])
        a_col = sb("a_col", [P, NH])
        c_col = sb("c_col", [P, NH])
        ident = sb("ident", [P, P])
        later = sb("later", [P, NS, P])
        not_later = sb("not_later", [P, NS, P])
        warm = sb("warm", [P, 1])
        half = sb("half", [P, NS])
        neg_half = sb("neg_half", [P, NS])
        x_tiles = sb("x_tiles", [P, PAIR, NH, S])
        x_t = sb("x_t", [P, PAIR, NH, S])
        x_res = sb("x_res", [P, PAIR, NS, H])
        adj_stage = sb("adj_stage", [P, PAIR, NS, S])
        adj_tiles = sb("adj_tiles", [P, PAIR, NS, S])
        mask = sb("mask", [P, PAIR, NS, SCORES])
        adj_t = sb("adj_t", [P, PAIR, NS, S])
        ht = parts("ht", [P, PAIR, NH, S])
        hl = parts("hl", [P, PAIR, NS, HL])
        y = sb("y", [P, PAIR, NS, H])
        h_full = sb("h_full", [P, NH, S])
        g = parts("g", [P, NH, 2 * S])
        hl_full = sb("hl_full", [P, NS, H])
        masked = sb("masked", [P, NS, SCORES])
        expd = sb("expd", [P, NS, S])
        p_full = sb("p_full", [P, NS, S])
        pt = parts("pt", [P, NS, S])
        z = sb("z", [P, NS, H])
        stats = sb("stats", [P, NS, 6])
        moments = sb("moments", [P, NS, 2])
        sum_eps = sb("sum_eps", [P, NS])
        std = sb("std", [P, NS])
        denom = sb("denom", [P, NS])
        inv_std = sb("inv_std", [P, NS])
        shift = sb("shift", [P, NS])
        out_stats = sb("out_stats", [P, NS, 6])
        out_moments = sb("out_moments", [P, NS, 2])
        out_var = sb("out_var", [P, PAIR, NS])
        out_inv = sb("out_inv", [P, PAIR, NS])
        out_mean = sb("out_mean", [P, PAIR, NS])
        out_shift = sb("out_shift", [P, PAIR, NS])

        proj = [bank(f"proj{c}", [P, 2 * S]) for c in range(NH)]
        score = [bank(f"score{j}", [P, 2 * S]) for j in range(NS)]
        ctx_ps = bank("ctx_ps", [P, NS, 2 * S])
        tr = bank("tr", [P, 2 * S])
        tr_bank = [tr[:, 0:S], ctx_ps[:, 0, 0:S], ctx_ps[:, 1, 0:S]]
        lin_bank = [[score[1][:, 0:H], ctx_ps[:, 0, 0:H], ctx_ps[:, 1, 0:H]], [proj[c][:, 0:H] for c in range(NH)]]

        w_loaded = [[sem(f"w{l}{n}_loaded") for n in ("right", "left", "lin")] for l in range(L)]
        bias_loaded = sem("bias_loaded")
        rows_loaded = sem("rows_loaded")
        x_loaded = [sem(f"x_loaded{p}") for p in range(PAIR)]
        adj_loaded = [sem(f"adj_loaded{p}") for p in range(PAIR)]
        adj_tiles_loaded = [sem(f"adj_tiles_loaded{p}") for p in range(PAIR)]
        x_res_loaded = [sem(f"x_res_loaded{p}") for p in range(PAIR)]
        stored = [sem(f"stored{p}") for p in range(PAIR)]
        stored_half = sem("stored_half")
        last_half_ready = sem("last_half_ready")
        consts_ready = sem("consts_ready")
        ident_filled = sem("ident_filled")
        ones_ready = sem("ones_ready")
        wt_done = sem("wt_done")
        wt_hi_ready = sem("wt_hi_ready")
        wt_lo_ready = sem("wt_lo_ready")
        w_hi_ready = sem("w_hi_ready")
        w_lo_ready = sem("w_lo_ready")
        ht_hi_ready = sem("ht_hi_ready")
        ht_lo_ready = sem("ht_lo_ready")
        g_done = sem("g_done")
        g_hi_ready = sem("g_hi_ready")
        g_lo_ready = sem("g_lo_ready")
        hl_done = sem("hl_done")
        hl_full_ready = sem("hl_full_ready")
        hl_hi_ready = sem("hl_hi_ready")
        hl_lo_ready = sem("hl_lo_ready")
        score_done = sem("score_done")
        masked_ready = sem("masked_ready")
        summed_ready = sem("summed_ready")
        exp_ready = sem("exp_ready")
        p_full_ready = sem("p_full_ready")
        p_hi_ready = sem("p_hi_ready")
        p_lo_ready = sem("p_lo_ready")
        ctx_done = sem("ctx_done")
        stats_ready = sem("stats_ready")
        sum_ready = sem("sum_ready")
        moments_ready = sem("moments_ready")
        std_ready = sem("std_ready")
        denom_ready = sem("denom_ready")
        inv_ready = sem("inv_ready")
        x_t_ready = sem("x_t_ready")
        adj_t_ready = sem("adj_t_ready")
        mask_ready = sem("mask_ready")
        transposed = sem("transposed")
        h_full_ready = sem("h_full_ready")
        shift_ready = sem("shift_ready")
        normed_ready = sem("normed_ready")
        centred_ready = sem("centred_ready")
        scaled_ready = sem("scaled_ready")
        affine_ready = sem("affine_ready")
        rectified_ready = sem("rectified_ready")
        resid_ready = sem("resid_ready")
        out_stats_ready = sem("out_stats_ready")
        out_moments_ready = sem("out_moments_ready")
        out_var_ready = sem("out_var_ready")
        out_inv_ready = sem("out_inv_ready")
        out_shift_ready = sem("out_shift_ready")
        out_ready = sem("out_ready")

        def element(dram, b):
            size = dram.shape[1] * dram.shape[2]
            flat = dram.rearrange("b s h -> (b s h)")[bass.ds(b * size, size)]
            return flat.rearrange("(n p h) -> p n h", p=P, h=dram.shape[2])

        def tiles(dram, b, to, quarter):
            size = dram.shape[1] * dram.shape[2]
            flat = dram.rearrange("b s h -> (b s h)")[bass.ds(b * size, size)]
            rows = flat.rearrange("(t r k q c) -> q r k t c", r=TILE, q=QUARTERS, c=TILE, k=dram.shape[2] // P)
            return (to[quarter * TILE:(quarter + 1) * TILE].rearrange("r k (t c) -> r k t c", c=TILE),
                    rows[quarter])

        def ahead(eng, dram, b, *counts):
            for value in (b * (dram.shape[1] * dram.shape[2] * 4), *counts):
                if not isinstance(value, int):
                    eng.to_reg(value)

        block = ctx.enter_context(nc.Block())

        def run_slots(eng, slot, first, last):
            first()
            for phase in (0, 1):
                slot(Slot(0, phase), at_start=(phase == 0), at_end=False)
            with eng.Fori(0, PAIRS - 1) as pair:
                for phase in (2, 3):
                    slot(Slot(pair, phase), at_start=False, at_end=False)
                for phase in (0, 1):
                    slot(Slot(pair + 1, phase), at_start=False, at_end=False)
            for phase in (2, 3):
                slot(Slot(PAIRS - 1, phase), at_start=False, at_end=(phase == 3))
            last()

        LAST = Slot(PAIRS - 1, PHASES - 1)

        @block.sync
        def _(sp):
            def load_x(b, p, quarters=range(QUARTERS)):
                for quarter in quarters:
                    sp.dma_start(*tiles(x, b, x_tiles[:, p], quarter)).then_inc(x_loaded[p], 16)

            def load_adj(b, p):
                for quarter in range(QUARTERS):
                    sp.dma_start(*tiles(adj, b, adj_tiles[:, p], quarter)).then_inc(adj_tiles_loaded[p], 16)
                sp.dma_start(adj_stage[:, p], element(adj, b)).then_inc(adj_loaded[p], 16)

            def load_w(l, n, w):
                sp.dma_start(w_stage[:, n], w[l].rearrange("(k p) h -> p k h", p=P)).then_inc(w_loaded[l][n], 16)

            def first():
                load_x(0, 0, range(NS))
                load_w(0, 0, w_right)
                load_w(0, 2, w_lin)
                load_adj(0, 0)
                load_x(1, 1)
                for l in range(L):
                    sp.dma_start(b_row[:, l, :], b_lin[l].partition_broadcast(P)).then_inc(bias_loaded, 16)
                sp.wait_ge(wt_done, NH)
                load_w(1, 2, w_lin)
                for n, w in enumerate((w_right, w_left)):
                    sp.wait_ge(w_lo_ready, (n + 1) * NH)
                    load_w(1, n, w)
                load_adj(1, 1)
                sp.dma_start(a_col[:, :], ln_a[0].rearrange("(k p) -> p k", p=P),
                             allow_slow_non_contiguous=True).then_inc(rows_loaded, 16)
                sp.dma_start(c_col[:, :], ln_b[0].rearrange("(k p) -> p k", p=P),
                             allow_slow_non_contiguous=True).then_inc(rows_loaded, 16)
                sp.dma_start(a_row[:, :], ln_a[1].partition_broadcast(P)).then_inc(rows_loaded, 16)
                sp.dma_start(c_row[:, :], ln_b[1].partition_broadcast(P)).then_inc(rows_loaded, 16)

            def store(s):
                ahead(sp, out, s.batch, s.done_batch(NS, NS))
                sp.wait_ge(out_ready, s.done_batch(NS, NS))
                sp.dma_start(element(out, s.batch), y[:, s.parity]).then_inc(stored[s.parity], 16)

            def load_residual(s):
                ahead(sp, x, s.batch, s.done_own(16, 0))
                sp.wait_ge(stored[s.parity], s.done_own(16, 0))
                sp.dma_start(x_res[:, s.parity], element(x, s.batch)).then_inc(x_res_loaded[s.parity], 16)

            def load_next(s):
                ahead(sp, x, s.batch + PAIR, s.done_batch(1, 1))
                ahead(sp, adj, s.batch + PAIR)
                sp.wait_ge(x_t_ready, s.done_batch(1, 1))
                sp.wait_ge(mask_ready, s.done_batch(1, 1))
                load_x(s.batch + PAIR, s.parity)
                load_adj(s.batch + PAIR, s.parity)

            first()
            for phase in (0, 1):
                load_next(Slot(0, phase))
                load_residual(Slot(0, phase))
            with sp.Fori(0, PAIRS - 2) as pair:
                for phase in (0, 1):
                    load_next(Slot(pair + 1, phase))
                    store(Slot(pair, phase))
                    load_residual(Slot(pair + 1, phase))
            for phase in (0, 1):
                store(Slot(PAIRS - 2, phase))
                load_residual(Slot(PAIRS - 1, phase))
            store(LAST.shift(-1))
            sp.wait_ge(last_half_ready, 1)
            sp.dma_start(out[LAST.batch, P:S], y[:, LAST.parity, 1]).then_inc(stored_half, 16)
            sp.wait_ge(stored[0], 16 * PAIRS)
            sp.wait_ge(stored[1], 16 * (PAIRS - 1))
            sp.wait_ge(stored_half, 2 * 16)

        @block.tensor
        def _(pe):
            def transpose_lin(l, blocks):
                pe.wait_ge(w_loaded[l][2], 16)
                for k in blocks:
                    if l == 1 and k < NS:
                        pe.wait_ge(hl_full_ready, k + 1)
                    elif l == 1:
                        pe.wait_ge(g_lo_ready, k + 1)
                    for o in range(NH):
                        last = nc.tensor.transpose(lin_bank[l][k][:, o * P:(o + 1) * P],
                                                   w_stage[:, 2, o, k * P:(k + 1) * P], ident[:, :])
                    last.then_inc(wt_done, 1)

            def transpose_z(s):
                pe.wait_ge(normed_ready, s.done_batch(NS, NS))
                pe.wait_ge(h_full_ready, s.done_batch(NH, 1 - NH))
                for k in range(NH):
                    for i in range(NS):
                        last = nc.tensor.transpose(tr_bank[k][:, i * P:(i + 1) * P],
                                                   z[:, i, k * P:(k + 1) * P], ident[:, :])
                    last.then_inc(transposed, 1)

            def project(s, c):
                if c < NS:
                    pe.wait_ge(hl_full_ready, s.done(NS, c + 1 - NS))
                if s.phase == 1 and isinstance(s.pair, int):
                    pe.wait_ge(wt_lo_ready, NH + c + 1)
                for w, at in ((wr, 0), (wl, S)):
                    for k in range(NH):
                        for n, (a, b) in enumerate(PASSES):
                            if c == 0 and at == 0 and n == 0:
                                pe.wait_ge(ht_hi_ready, s.done(NH, k + 1))
                            if c == 0 and n < 2:
                                part_ready = w_hi_ready if a == "hi" else w_lo_ready
                                pe.wait_ge(part_ready, (2 * s.layer + at // S) * NH + k + 1)
                            if c == 0 and at == 0 and n == 2:
                                pe.wait_ge(ht_lo_ready, s.done(NH, k + 1))
                            last = nc.tensor.matmul(proj[c][:, at:at + S],
                                                    w[a][:, s.layer, k, c * P:(c + 1) * P],
                                                    ht[b][:, s.parity, k, :],
                                                    start=(k == 0 and n == 0), stop=(k == NH - 1 and n == 2))
                last.then_inc(g_done, 1)

            def linear(s, i):
                pe.wait_ge(g_lo_ready, s.done(NH, i + 1))
                for k in range(NH):
                    if i == 0:
                        pe.wait_ge(wt_lo_ready, NH * s.layer + k + 1)
                    for n, (a, b) in enumerate(PASSES):
                        last = nc.tensor.matmul(proj[i][:, 0:H], ht[a][:, s.parity, k, i * P:(i + 1) * P],
                                                wt[b][:, s.layer, k, :],
                                                start=(k == 0 and n == 0), stop=(k == NH - 1 and n == 2))
                last.then_inc(hl_done, 1)

            def scores(s, j):
                if j == 0:
                    pe.wait_ge(g_lo_ready, s.done(NH, NH))
                pe.wait_ge(masked_ready, s.done(NS, j + 1 - NS))
                for k in range(NH):
                    for n, (a, b) in enumerate(PASSES):
                        last = nc.tensor.matmul(score[j][:, 0:SCORES], ht[a][:, s.parity, k, j * P:(j + 1) * P],
                                                g[b][:, k, j * P:j * P + SCORES],
                                                start=(k == 0 and n == 0), stop=(k == NH - 1 and n == 2))
                last.then_inc(score_done, 1)

            def context(s):
                pe.wait_ge(hl_lo_ready, s.done(NS, NS))
                before = s.shift(-1)
                if before.layer == 0:
                    pe.wait_ge(normed_ready, before.done_batch(NS, NS))
                elif not (isinstance(s.pair, int) and s.pair == 0 and s.phase == 0):
                    pe.wait_ge(centred_ready, before.done_batch(NS, NS))
                nxt = s.shift(1)
                if s is not LAST and nxt.layer == 1:
                    pe.wait_ge(h_full_ready, nxt.done_batch(NH, NH))
                for j in range(NS):
                    pe.wait_ge(p_lo_ready, s.done(NS, j + 1))
                    for i in range(NS):
                        q = i if j == 0 else 1 - i
                        for n, (a, b) in enumerate(PASSES):
                            wide = HL if b == "hi" else H
                            last = nc.tensor.matmul(ctx_ps[:, i, 0:wide], pt[a][:, j, q * P:(q + 1) * P],
                                                    hl[b][:, s.parity, j, 0:wide],
                                                    start=(j == 0 and n == 0), stop=(j == NS - 1 and n == 2))
                        if j == NS - 1:
                            last.then_inc(ctx_done, 1)

            def slot(s, at_start, at_end):
                prev, nxt = s.shift(-1), s.shift(1)
                project(s, 0)
                project(s, 1)
                if at_start:
                    transpose_lin(0, range(NH))
                if not at_start:
                    context(prev)
                project(s, 2)
                linear(s, 0)
                if not at_end and nxt.layer == 1:
                    transpose_z(nxt)
                linear(s, 1)
                if at_start:
                    transpose_lin(1, (0,))
                scores(s, 0)
                if at_start:
                    transpose_lin(1, (1, 2))
                scores(s, 1)

            def first():
                pe.wait_ge(consts_ready, 1)
                for _ in range(WARM_UP):
                    nc.tensor.transpose(tr[:, 0:P], ident[:, :], ident[:, :])
                pe.wait_ge(ones_ready, PAIR * NS)

            def last():
                context(LAST)

            run_slots(pe, slot, first, last)

        @block.scalar
        def _(act):
            def take_w(l, n):
                w = (wr, wl)[n]
                act.wait_ge(w_loaded[l][n], 16)
                for k in range(NH):
                    nc.scalar.copy(w["hi"][:, l, k], w_stage[:, n, k]).then_inc(w_hi_ready, 1)

            def take_lin(l, blocks):
                for k in blocks:
                    act.wait_ge(wt_done, NH * l + k + 1)
                    nc.scalar.copy(wt["hi"][:, l, k, :], lin_bank[l][k]).then_inc(wt_hi_ready, 1)

            def take_h(s):
                act.wait_ge(score_done, s.done(NS, -NS))
                for k in range(NH):
                    if s.layer == 0:
                        act.wait_ge(x_t_ready, s.done_batch(1, 1))
                        nc.scalar.copy(ht["hi"][:, s.parity, k, :], x_t[:, s.parity, k, :]).then_inc(ht_hi_ready, 1)
                    else:
                        act.wait_ge(transposed, s.done_batch(NH, k + 1))
                        nc.scalar.activation(ht["hi"][:, s.parity, k, :], tr_bank[k], ACT.Relu,
                                             bias=c_col[:, k:k + 1],
                                             scale=a_col[:, k:k + 1]).then_inc(ht_hi_ready, 1)
                        act.wait_ge(ht_lo_ready, s.done(NH, k + 1 - NH))
                        nc.scalar.activation(h_full[:, k, :], tr_bank[k], ACT.Relu, bias=c_col[:, k:k + 1],
                                             scale=a_col[:, k:k + 1]).then_inc(h_full_ready, 1)

            def take_g(s, c):
                act.wait_ge(g_done, s.done(NH, c + 1))
                act.wait_ge(score_done, s.done(NS, 0))
                nc.scalar.copy(g["hi"][:, c, :], proj[c][:, :]).then_inc(g_hi_ready, 1)

            def take_hl(s, i):
                act.wait_ge(hl_full_ready, s.done(NS, i + 1))
                act.wait_ge(ctx_done, s.done(NS, -NS))
                nc.scalar.copy(hl["hi"][:, s.parity, i, 0:H], hl_full[:, i, :]).then_inc(hl_hi_ready, 1)

            def exponent(s, j):
                act.wait_ge(summed_ready, s.done(NS, j + 1))
                act.wait_ge(p_full_ready, s.done(NS, j + 1 - NS))
                nc.scalar.activation(expd[:, j, :], masked[:, j, 0:S], ACT.Exp,
                                     scale=1.0 / TEMPER).then_inc(exp_ready, 1)

            def normalise(s):
                act.wait_ge(transposed, s.done_batch(NH, 0))
                for i in range(NS):
                    act.wait_ge(shift_ready, s.done_batch(NS, i + 1))
                    nc.scalar.activation(z[:, i, :], ctx_ps[:, i, 0:H], ACT.Identity, bias=shift[:, i:i + 1],
                                         scale=inv_std[:, i:i + 1]).then_inc(normed_ready, 1)

            def scale(s):
                for i in range(NS):
                    yi = y[:, s.parity, i, :]
                    act.wait_ge(centred_ready, s.done_batch(NS, i + 1))
                    act.wait_ge(inv_ready, s.done(NS, i + 1))
                    nc.scalar.activation(yi, yi, ACT.Identity, scale=inv_std[:, i:i + 1]).then_inc(scaled_ready, 1)

            def rectify(s):
                for i in range(NS):
                    yi = y[:, s.parity, i, :]
                    act.wait_ge(affine_ready, s.done_batch(NS, i + 1))
                    nc.scalar.activation(yi, yi, ACT.Relu).then_inc(rectified_ready, 1)

            def finish_block(s, i):
                nc.scalar.activation(y[:, s.parity, i, :], y[:, s.parity, i, :], ACT.Identity,
                                     bias=out_shift[:, s.parity, i:i + 1],
                                     scale=out_inv[:, s.parity, i:i + 1]).then_inc(out_ready, 1)

            def finish(s):
                act.wait_ge(out_shift_ready, s.done_batch(1, 1))
                for i in range(NS):
                    finish_block(s, i)

            def slot(s, at_start, at_end):
                prev, before, nxt = s.shift(-1), s.shift(-2), s.shift(1)
                output_before = before.layer == 1 and not (isinstance(s.pair, int) and s.pair == 0)
                if not at_start:
                    exponent(prev, 1)
                take_g(s, 0)
                if output_before:
                    rectify(before)
                if at_start:
                    take_lin(0, range(NH))
                take_g(s, 1)
                if isinstance(s.pair, int) and s.pair == 0 and s.phase == 1:
                    take_w(1, 1)
                    act.wait_ge(rows_loaded, 4 * 16)
                if output_before and s.phase == 1:
                    finish(before.shift(-1))
                if not at_start and prev.layer == 0:
                    normalise(prev)
                take_g(s, 2)
                if not at_start and prev.layer == 1:
                    scale(prev)
                if not at_end:
                    take_h(nxt)
                take_hl(s, 0)
                take_hl(s, 1)
                if at_start:
                    take_lin(1, (0,))
                exponent(s, 0)
                if output_before and s.phase == 1:
                    finish(before)
                if at_start:
                    take_lin(1, (1, 2))
                    take_w(1, 0)

            def first():
                for quarter in range(NS, QUARTERS):
                    act.dma_start(*tiles(x, 0, x_tiles[:, 0], quarter)).then_inc(x_loaded[0], 16)
                act.dma_start(w_stage[:, 1], w_left[0].rearrange("(k p) h -> p k h", p=P)).then_inc(w_loaded[0][1], 16)
                act.wait_ge(consts_ready, 1)
                nc.scalar.copy(warm[:, :], ident[:, 0:1])
                take_h(Slot(0, 0))
                for n in range(2):
                    take_w(0, n)

            def last():
                exponent(LAST, 1)
                rectify(LAST.shift(-1))
                finish(LAST.shift(-1))
                act.wait_ge(out_shift_ready, LAST.done_batch(1, 1))
                finish_block(LAST, 0)
                act.wait_ge(out_ready, LAST.done_batch(NS, 1))
                act.dma_start(out[LAST.batch, 0:P], y[:, LAST.parity, 0]).then_inc(stored_half, 16)

            run_slots(act, slot, first, last)

        @block.vector
        def _(dve):
            def split_w(l, n):
                w = (wr, wl)[n]
                for k in range(NH):
                    dve.wait_ge(w_hi_ready, (2 * l + n) * NH + k + 1)
                    if l == 1:
                        dve.wait_ge(w_lo_ready, 3 * NH)
                    nc.vector.tensor_tensor(w["lo"][:, l, k], w_stage[:, n, k], w["hi"][:, l, k].bitcast(F32),
                                            ALU.subtract).then_inc(w_lo_ready, 1)

            def split_lin(l, blocks):
                for k in blocks:
                    dve.wait_ge(wt_hi_ready, NH * l + k + 1)
                    nc.vector.tensor_tensor(wt["lo"][:, l, k, :], lin_bank[l][k], wt["hi"][:, l, k, :].bitcast(F32),
                                            ALU.subtract).then_inc(wt_lo_ready, 1)

            def transpose_x(s):
                dve.wait_ge(x_loaded[s.parity], s.done_own(16 * QUARTERS, 16 * QUARTERS))
                nc.vector.transpose(x_t[:, s.parity].rearrange("p k s -> p (k s)"),
                                    x_tiles[:, s.parity].rearrange("p k s -> p (k s)")).then_inc(x_t_ready, 1)

            def transpose_adj(s):
                dve.wait_ge(adj_tiles_loaded[s.parity], s.done_own(16 * QUARTERS, 16 * QUARTERS))
                for j in range(NS):
                    for n in range(NS):
                        i = n if j == 0 else 1 - n
                        nc.vector.transpose(adj_t[:, s.parity, j, n * P:(n + 1) * P],
                                            adj_tiles[:, s.parity, j, i * P:(i + 1) * P]).then_inc(adj_t_ready, 1)

            def split_h(s):
                for k in range(NH):
                    hi, lo = (ht[a][:, s.parity, k, :] for a in ("hi", "lo"))
                    if s.layer == 1:
                        dve.wait_ge(h_full_ready, s.done_batch(NH, k + 1))
                    dve.wait_ge(ht_hi_ready, s.done(NH, k + 1))
                    nc.vector.tensor_tensor(lo, h_full[:, k, :] if s.layer else x_t[:, s.parity, k, :], hi.bitcast(F32),
                                            ALU.subtract).then_inc(ht_lo_ready, 1)

            def split_g(s, c):
                dve.wait_ge(g_hi_ready, s.done(NH, c + 1))
                nc.vector.tensor_tensor(g["lo"][:, c, :], proj[c][:, :], g["hi"][:, c, :].bitcast(F32),
                                        ALU.subtract).then_inc(g_lo_ready, 1)

            def add_bias(s, i):
                dve.wait_ge(hl_done, s.done(NS, i + 1))
                dve.wait_ge(hl_lo_ready, s.done(NS, i + 1 - NS))
                nc.vector.tensor_tensor(hl_full[:, i, :], proj[i][:, 0:H], b_row[:, s.layer, :],
                                        ALU.add).then_inc(hl_full_ready, 1)

            def mask_scores(s, j):
                dve.wait_ge(score_done, s.done(NS, j + 1))
                dve.wait_ge(mask_ready, s.done_batch(1, 1))
                dve.wait_ge(exp_ready, s.done(NS, j + 1 - NS))
                nc.vector.tensor_tensor(masked[:, j, :], score[j][:, 0:SCORES], mask[:, s.parity, j, :],
                                        ALU.mult).then_inc(masked_ready, 1)
                dve.wait_ge(masked_ready, s.done(NS, j + 1))
                nc.vector.tensor_tensor(masked[:, j, 0:P], masked[:, j, 0:P], masked[:, j, 2 * P:3 * P],
                                        ALU.add).then_inc(summed_ready, 1)

            def weigh(s, j):
                dve.wait_ge(exp_ready, s.done(NS, j + 1))
                nc.vector.tensor_tensor(p_full[:, j, :], expd[:, j, :], adj_t[:, s.parity, j, :],
                                        ALU.mult).then_inc(p_full_ready, 1)

            def take_p(s, j):
                dve.wait_ge(p_full_ready, s.done(NS, j + 1))
                dve.wait_ge(ctx_done, s.done(NS, 0))
                nc.vector.tensor_copy(pt["hi"][:, j, :], p_full[:, j, :]).then_inc(p_hi_ready, 1)

            def split_p(s, j):
                dve.wait_ge(p_hi_ready, s.done(NS, j + 1))
                nc.vector.tensor_tensor(pt["lo"][:, j, :], p_full[:, j, :], pt["hi"][:, j, :].bitcast(F32),
                                        ALU.subtract).then_inc(p_lo_ready, 1)

            def norm_scalars(s):
                for i in range(NS):
                    dve.wait_ge(ctx_done, s.done(NS, i + 1))
                    nc.vector.bn_stats(stats[:, i, :], ctx_ps[:, i, 0:H]).then_inc(stats_ready, 1)
                    dve.wait_ge(stats_ready, s.done(NS, i + 1))
                    nc.vector.tensor_scalar(sum_eps[:, i:i + 1], ctx_ps[:, i, H:H + 1], LN_EPS, LN_EPS * SUM_EPS,
                                            ALU.mult, ALU.add).then_inc(sum_ready, 1)
                    nc.vector.bn_aggr(moments[:, i, :], stats[:, i, :]).then_inc(moments_ready, 1)
                if s.layer == 1:
                    centre(s)
                for i in range(NS):
                    dve.wait_ge(sum_ready, s.done(NS, i + 1))
                    dve.wait_ge(std_ready, s.done(NS, i + 1))
                    if s.shift(-1).layer == 1 and not (isinstance(s.pair, int) and s.pair == 0):
                        dve.wait_ge(scaled_ready, s.shift(-1).done_batch(NS, NS))
                    nc.vector.scalar_tensor_tensor(denom[:, i:i + 1], std[:, i:i + 1], DDOF, sum_eps[:, i:i + 1],
                                                   ALU.mult, ALU.add).then_inc(denom_ready, 1)
                    dve.wait_ge(denom_ready, s.done(NS, i + 1))
                    nc.vector.reciprocal(inv_std[:, i:i + 1], denom[:, i:i + 1]).then_inc(inv_ready, 1)
                    if s.layer == 0:
                        dve.wait_ge(inv_ready, s.done(NS, i + 1))
                        nc.vector.scalar_tensor_tensor(shift[:, i:i + 1], moments[:, i, 0:1], -1.0,
                                                       inv_std[:, i:i + 1], ALU.mult,
                                                       ALU.mult).then_inc(shift_ready, 1)

            def centre(s):
                dve.wait_ge(moments_ready, s.done(NS, NS))
                dve.wait_ge(x_res_loaded[s.parity], s.done_own(16, 16))
                dve.wait_ge(rows_loaded, 4 * 16)
                for i in range(NS):
                    nc.vector.scalar_tensor_tensor(y[:, s.parity, i, :], ctx_ps[:, i, 0:H], moments[:, i, 0:1],
                                                   a_row[:, :], ALU.subtract, ALU.mult).then_inc(centred_ready, 1)

            def scale_last(s):
                for i in range(NS):
                    yi = y[:, s.parity, i, :]
                    dve.wait_ge(inv_ready, s.done(NS, i + 1))
                    dve.wait_ge(centred_ready, s.done_batch(NS, i + 1))
                    nc.vector.scalar_tensor_tensor(yi, yi, inv_std[:, i:i + 1], c_row[:, :], ALU.mult,
                                                   ALU.add).then_inc(affine_ready, 1)

            def add_residual_last(s):
                for i in range(NS):
                    yi = y[:, s.parity, i, :]
                    dve.wait_ge(affine_ready, s.done_batch(NS, i + 1))
                    nc.vector.scalar_tensor_tensor(yi, yi, 0.0, x_res[:, s.parity, i, :], ALU.max,
                                                   ALU.add).then_inc(resid_ready, 1)

            def measure(s, i):
                dve.wait_ge(resid_ready, s.done_batch(NS, i + 1))
                nc.vector.bn_stats(out_stats[:, i, :], y[:, s.parity, i, :]).then_inc(out_stats_ready, 1)

            def out_variance(s):
                for i in range(NS):
                    nc.vector.bn_aggr(out_moments[:, i, :], out_stats[:, i, :]).then_inc(out_moments_ready, 1)
                dve.wait_ge(out_moments_ready, s.done_batch(NS, NS))
                nc.vector.tensor_scalar(out_var[:, s.parity, :], out_moments[:, :, 1], OUT_EPS, None,
                                        ALU.add).then_inc(out_var_ready, 1)
                nc.vector.tensor_copy(out_mean[:, s.parity, :], out_moments[:, :, 0]).then_inc(out_var_ready, 1)

            def out_scalars(s):
                dve.wait_ge(out_inv_ready, s.done_batch(1, 1))
                nc.vector.scalar_tensor_tensor(out_shift[:, s.parity, :], out_mean[:, s.parity, :], -1.0,
                                               out_inv[:, s.parity, :], ALU.mult,
                                               ALU.mult).then_inc(out_shift_ready, 1)

            def slot(s, at_start, at_end):
                prev, before, nxt = s.shift(-1), s.shift(-2), s.shift(1)
                output_before = before.layer == 1 and not (isinstance(s.pair, int) and s.pair == 0)
                if not at_start:
                    mask_scores(prev, 1)
                    weigh(prev, 0)
                    take_p(prev, 0)
                    weigh(prev, 1)
                    split_p(prev, 0)
                    take_p(prev, 1)
                    split_p(prev, 1)
                split_g(s, 0)
                if at_start:
                    split_lin(0, range(NH))
                if s.layer == 0:
                    transpose_adj(s)
                split_g(s, 1)
                if output_before and s.phase == 1:
                    out_scalars(before.shift(-1))
                if not at_start:
                    norm_scalars(prev)
                if isinstance(s.pair, int) and s.pair == 0 and s.phase == 1:
                    split_w(1, 1)
                if at_start:
                    transpose_x(nxt)
                split_g(s, 2)
                more = s.phase == PAIR and not (isinstance(s.pair, int) and s.pair == PAIRS - 1)
                if more:
                    transpose_x(s.shift(2))
                if at_start:
                    dve.wait_ge(bias_loaded, L * 16)
                add_bias(s, 0)
                if output_before:
                    for i in range(NS):
                        measure(before, i)
                if more:
                    transpose_x(s.shift(3))
                if output_before:
                    dve.wait_ge(out_stats_ready, before.done_batch(NS, NS))
                x_is_next = not at_end and nxt.layer == 0 and not at_start
                if x_is_next:
                    split_h(nxt)
                add_bias(s, 1)
                if not at_end and not x_is_next:
                    split_h(nxt)
                if output_before and s.phase == 1:
                    out_variance(before)
                if at_start:
                    split_lin(1, (0,))
                mask_scores(s, 0)
                if output_before and s.phase == 0:
                    out_variance(before)
                if output_before and s.phase == 1:
                    out_scalars(before)
                if at_start:
                    split_lin(1, (1, 2))

            def first():
                ones = [hl["hi"][:, p, i, H:HL].bitcast(F32) for p in range(PAIR) for i in range(NS)]
                for t in ones:
                    nc.vector.memset(t, 1.0).then_inc(ones_ready, 1)
                transpose_x(Slot(0, 0))
                split_h(Slot(0, 0))
                for n in range(2):
                    split_w(0, n)

            def last():
                before = LAST.shift(-1)
                dve.wait_ge(rows_loaded, 4 * 16)
                mask_scores(LAST, 1)
                weigh(LAST, 0)
                take_p(LAST, 0)
                weigh(LAST, 1)
                split_p(LAST, 0)
                take_p(LAST, 1)
                split_p(LAST, 1)
                for i in range(NS):
                    measure(before, i)
                dve.wait_ge(out_stats_ready, before.done_batch(NS, NS))
                out_variance(before)
                norm_scalars(LAST)
                out_scalars(before)
                scale_last(LAST)
                add_residual_last(LAST)
                for i in range(NS):
                    measure(LAST, i)
                dve.wait_ge(out_stats_ready, LAST.done_batch(NS, NS))
                out_variance(LAST)
                out_scalars(LAST)
                dve.wait_ge(out_shift_ready, LAST.done_batch(1, 1))
                yi = y[:, LAST.parity, 1, :]
                nc.vector.tensor_scalar(yi, yi, out_inv[:, LAST.parity, 1:2], out_shift[:, LAST.parity, 1:2],
                                        ALU.mult, ALU.add).then_inc(last_half_ready, 1)

            run_slots(dve, slot, first, last)

        @block.gpsimd
        def _(pool):
            def deviation(s):
                for i in range(NS):
                    pool.wait_ge(moments_ready, s.done(NS, i + 1))
                    pool.wait_ge(denom_ready, s.done(NS, i + 1 - NS))
                    nc.gpsimd.tensor_tensor(std[:, i:i + 1], moments[:, i, 1:2], half[:, i:i + 1],
                                            ALU.pow).then_inc(std_ready, 1)

            def out_deviation(s):
                pool.wait_ge(out_var_ready, s.done_batch(2, 2))
                nc.gpsimd.tensor_tensor(out_inv[:, s.parity, :], out_var[:, s.parity, :], neg_half[:, :],
                                        ALU.pow).then_inc(out_inv_ready, 1)

            def add_residual(s, i):
                yi = y[:, s.parity, i, :]
                pool.wait_ge(rectified_ready, s.done_batch(NS, i + 1))
                nc.gpsimd.tensor_tensor(yi, yi, x_res[:, s.parity, i, :], ALU.add).then_inc(resid_ready, 1)

            def split_hl(s, i):
                pool.wait_ge(hl_hi_ready, s.done(NS, i + 1))
                nc.gpsimd.tensor_tensor(hl["lo"][:, s.parity, i, 0:H], hl_full[:, i, :],
                                        hl["hi"][:, s.parity, i, 0:H].bitcast(F32),
                                        ALU.subtract).then_inc(hl_lo_ready, 1)

            def make_mask(s):
                m, a, at = mask[:, s.parity], adj_stage[:, s.parity], adj_t[:, s.parity]
                pool.wait_ge(adj_t_ready, s.done_batch(4, 4))
                pool.wait_ge(adj_loaded[s.parity], s.done_own(16, 16))
                pool.wait_ge(masked_ready, s.done(NS, -NS))
                diagonal = a.rearrange("p n (m q) -> p (n m) q", q=P)[:, 0::NS + 1, :]
                nc.gpsimd.tensor_tensor(m[:, :, 0:P], diagonal, later[:, :, :], ALU.mult)
                nc.gpsimd.tensor_tensor(m[:, :, 2 * P:3 * P], at[:, :, 0:P], not_later[:, :, :], ALU.mult)
                nc.gpsimd.tensor_copy(m[:, 0, P:2 * P], a[:, 0, P:2 * P])
                nc.gpsimd.tensor_copy(m[:, 1, P:2 * P], at[:, 1, P:2 * P]).then_inc(mask_ready, 1)

            def add_offset(s, i):
                yi = y[:, s.parity, i, :]
                pool.wait_ge(rows_loaded, 4 * 16)
                pool.wait_ge(scaled_ready, s.done_batch(NS, i + 1))
                nc.gpsimd.tensor_tensor(yi, yi, c_row[:, :], ALU.add).then_inc(affine_ready, 1)

            def slot(s, at_start, at_end):
                prev, before, nxt = s.shift(-1), s.shift(-2), s.shift(1)
                output = not at_start and prev.layer == 1
                output_before = before.layer == 1 and not (isinstance(s.pair, int) and s.pair == 0)
                if output_before:
                    pool.wait_ge(p_lo_ready, prev.done(NS, NS))
                    for i in range(NS):
                        add_residual(before, i)
                if not at_start:
                    deviation(prev)
                if s.layer == 0:
                    if not at_start:
                        if prev.layer == 0:
                            pool.wait_ge(shift_ready, prev.done_batch(NS, NS))
                        else:
                            pool.wait_ge(inv_ready, prev.done(NS, NS))
                    make_mask(s)
                if output:
                    for i in range(NS):
                        add_offset(prev, i)
                if output_before and s.phase == 1:
                    out_deviation(before)
                if not at_end and not at_start:
                    pool.wait_ge(ht_lo_ready, nxt.done(NH, NH))
                for i in range(NS):
                    split_hl(s, i)
                if output_before and s.phase == 0:
                    out_deviation(before)
                if at_start:
                    for k in range(NH):
                        pool.wait_ge(w_hi_ready, 2 * NH + k + 1)
                        nc.gpsimd.tensor_tensor(wr["lo"][:, 1, k], w_stage[:, 0, k], wr["hi"][:, 1, k].bitcast(F32),
                                                ALU.subtract).then_inc(w_lo_ready, 1)

            def first():
                nc.gpsimd.memset(ident[:, :], 1.0).then_inc(ident_filled, 1)
                pool.wait_ge(ident_filled, 1)
                nc.gpsimd.affine_select(out=ident[:, :], in_=ident[:, :], pattern=[[-1, P]], compare_op=ALU.is_equal,
                                        fill=0.0, base=0, channel_multiplier=1).then_inc(consts_ready, 1)
                nc.gpsimd.memset(half[:, :], 0.5)
                nc.gpsimd.memset(neg_half[:, :], -0.5)
                nc.gpsimd.memset(later[:, :, :], 1.0).then_inc(ident_filled, 1)
                nc.gpsimd.memset(not_later[:, :, :], 1.0).then_inc(ident_filled, 1)
                pool.wait_ge(ident_filled, 3)
                for j in range(NS):
                    nc.gpsimd.affine_select(out=later[:, j, :], in_=later[:, j, :], pattern=[[1, P]],
                                            compare_op=ALU.is_gt, fill=0.0, base=0,
                                            channel_multiplier=-1).then_inc(consts_ready, 1)
                    nc.gpsimd.affine_select(out=not_later[:, j, :], in_=not_later[:, j, :], pattern=[[-1, P]],
                                            compare_op=ALU.is_ge, fill=0.0, base=0,
                                            channel_multiplier=1).then_inc(consts_ready, 1)
                pool.wait_ge(consts_ready, 1 + 2 * NS)

            def last():
                for i in range(NS):
                    add_residual(LAST.shift(-1), i)
                out_deviation(LAST.shift(-1))
                deviation(LAST)
                out_deviation(LAST)

            run_slots(pool, slot, first, last)


_INS = ["x", "adj", "L0_gnn_W_left", "L0_gnn_W_right", "L0_gnn_W_lin", "L0_gnn_b_lin", "L0_gnn_ln_a", "L0_gnn_ln_b"]


def kernel(**inputs):
    import numpy as _np
    import concourse.bacc as _bacc
    from concourse import mybir as _mybir
    from concourse.bass_utils import run_bass_kernel_spmd as _run

    nc = _bacc.Bacc("TRN2", target_bir_lowering=False, num_devices=1)
    arrays, args = {}, []
    for name in _INS:
        a = _np.ascontiguousarray(inputs[name])
        arrays[f"in_{name}"] = a
        args.append(nc.dram_tensor(f"in_{name}", a.shape, _mybir.dt.from_np(a.dtype), kind="ExternalInput").ap())
    out = nc.dram_tensor("out_0", inputs["x"].shape, _mybir.dt.float32, kind="ExternalOutput").ap()
    build(nc, *args, out)
    r = _run(nc, [arrays], core_ids=[0])
    return r.results[0]["out_0"]
```
